# Optimizing a Trainium2 kernel written in Bass

```python
import numpy as np
import jax
import jax.numpy as jnp

def _softmax(x, axis=-1):
    return jax.nn.softmax(x, axis=axis)
def _gelu(x):
    return jax.nn.gelu(x, approximate=True)
def _silu(x):
    return jax.nn.silu(x)
def _sigmoid(x):
    return jax.nn.sigmoid(x)
def _layernorm(x, axis=-1, eps=1e-5):
    m = jnp.mean(x, axis=axis, keepdims=True)
    v = jnp.var(x, axis=axis, keepdims=True)
    return (x - m) / jnp.sqrt(v + eps)
def _scatter_add(tgt, idx, src, axis=0):
    return tgt.at[idx].add(src)
def _segment_sum(src, seg, n):
    return jax.ops.segment_sum(src, seg, n)

kernel_name = 'mk_adj_preln_d2_adj_512_28f7ba'

def setup_inputs(seed: int = 0):
    np.random.seed(seed)
    _w = jnp.asarray
    def _rec_inputs():
        import jax
        import jax.numpy as jnp
        _gk = jax.random.key(seed)
        x = -0.001547 + 1.001 * jax.random.normal(jax.random.fold_in(_gk, 1), (128, 128, 512), jnp.float32)
        _w = (1.0 + jnp.arange(128, dtype=jnp.float32)) ** -0.5
        _w = _w / _w.mean()
        _pij = jnp.clip(0.125 * _w[:, None] * _w[None, :], 0.0, 1.0)
        _a = jax.random.uniform(jax.random.fold_in(_gk, 2), (128, 128)) < _pij
        _a = jnp.logical_or(_a, jnp.swapaxes(_a, -1, -2))
        _a = jnp.logical_or(_a, jnp.eye(128, dtype=bool))
        _af = _a.astype(jnp.float32)
        _af = _af * jax.random.uniform(jax.random.fold_in(_gk, 3), (128, 128), jnp.float32, 0.05, 0.237401)
        adj = _af
        return x, adj
    x, adj = _rec_inputs()
    def _L0_gnn_setup():
        import jax, jax.numpy as jnp
        import numpy as np
        key = jax.random.key(seed)
        k1, k2, k3, k4 = jax.random.split(key, 4)
        B, D, N = (4, 128, 512)
        scale = 1.0 / np.sqrt(2 * D)
        x = jax.random.normal(k1, (B, D, N), dtype=jnp.float32)
        W1 = jax.random.normal(k2, (D, D), dtype=jnp.float32) * scale
        W2 = jax.random.normal(k3, (D, D), dtype=jnp.float32) * scale
        b = jax.random.normal(k4, (D,), dtype=jnp.float32) * scale
        return {'x': x, 'W1': W1, 'W2': W2, 'b': b}
    _L0_gnn_all = _L0_gnn_setup()
    _L0_gnn_in = {k: v for k, v in _L0_gnn_all.items() if k in ('b', )}
    del _L0_gnn_all

    def _L1_gnn_setup():
        import jax, jax.numpy as jnp
        import numpy as np
        B, N, D = (4, 2048, 512)
        H, HD = (8, 64)
        key = jax.random.key(seed)
        ks = jax.random.split(key, 6)
        x = jax.random.normal(ks[0], (B, N, D), dtype=jnp.float32)
        adj = (jax.random.uniform(ks[1], (N, N)) < 0.1).astype(jnp.float32)
        adj = jnp.maximum(adj, jnp.eye(N, dtype=jnp.float32))
        s = 0.02
        Wq = jax.random.normal(ks[2], (D, H * HD), dtype=jnp.float32) * s
        Wk = jax.random.normal(ks[3], (D, H * HD), dtype=jnp.float32) * s
        Wv = jax.random.normal(ks[4], (D, H * HD), dtype=jnp.float32) * s
        bq = jnp.zeros((H * HD,), dtype=jnp.float32)
        bk = jnp.zeros((H * HD,), dtype=jnp.float32)
        bv = jnp.zeros((H * HD,), dtype=jnp.float32)
        return {'x': x, 'adj': adj, 'Wq': Wq, 'bq': bq, 'Wk': Wk, 'bk': bk, 'Wv': Wv, 'bv': bv}
    _L1_gnn_all = _L1_gnn_setup()
    _L1_gnn_in = {k: v for k, v in _L1_gnn_all.items() if k in ('Wq', 'bq', 'Wk', 'bk', 'Wv', 'bv', )}
    del _L1_gnn_all

    return {
        "x": x,
        "adj": adj,
        "L0_gnn_b": _L0_gnn_in["b"],
        "L1_gnn_Wq": _L1_gnn_in["Wq"],
        "L1_gnn_bq": _L1_gnn_in["bq"],
        "L1_gnn_Wk": _L1_gnn_in["Wk"],
        "L1_gnn_bk": _L1_gnn_in["bk"],
        "L1_gnn_Wv": _L1_gnn_in["Wv"],
        "L1_gnn_bv": _L1_gnn_in["bv"],
    }

def reference(x, adj, L0_gnn_b, L1_gnn_Wq, L1_gnn_bq, L1_gnn_Wk, L1_gnn_bk, L1_gnn_Wv, L1_gnn_bv):
    import jax
    import jax.numpy as jnp
    def _L0_gnn_ref(x, W1, W2, b):
        import jax, jax.numpy as jnp
        import numpy as np
        A = jnp.einsum('od,bdn->bon', W1, x)
        C = jnp.einsum('od,bdn->bon', W2, x) + b[None, :, None]
        pre = A[:, :, None, :] + (C - A)[:, :, :, None]
        out = jnp.max(jax.nn.relu(pre), axis=-1)
        return out

    def _L1_gnn_ref(x, adj, Wq, bq, Wk, bk, Wv, bv):
        import jax, jax.numpy as jnp
        import numpy as np
        B, N, D = (4, 2048, 512)
        H, HD = (8, 64)
        b, n, _ = x.shape
        q = (x @ Wq + bq).reshape(b, n, H, HD)
        k = (x @ Wk + bk).reshape(b, n, H, HD)
        v = (x @ Wv + bv).reshape(b, n, H, HD)
        scores = jnp.einsum('bihd,bjhd->bhij', q, k) / jnp.sqrt(jnp.float32(HD))
        mask = jnp.where(adj == 0, jnp.float32(-1000000000.0), jnp.float32(0.0))
        scores = scores + mask[None, None, :, :]
        weights = jax.nn.softmax(scores, axis=-1)
        out = jnp.einsum('bhij,bjhd->bihd', weights, v)
        return out.reshape(b, n, H * HD)

    h = jnp.maximum(_layernorm(x, axis=-1), 0.0)
    x = x + _L0_gnn_ref(h, adj, adj, L0_gnn_b)
    h = jnp.maximum(_layernorm(x, axis=-1), 0.0)
    x = x + _L1_gnn_ref(h, adj, L1_gnn_Wq, L1_gnn_bq, L1_gnn_Wk, L1_gnn_bk, L1_gnn_Wv, L1_gnn_bv)
    return x


_drawn_inputs = setup_inputs


def setup_inputs(seed=0):
    import zlib

    import numpy as np

    out = dict(_drawn_inputs(seed))
    spreads = {'L1_gnn_bq': (0.0, 0.8), 'L1_gnn_bk': (0.0, 0.8), 'L1_gnn_bv': (0.0, 0.302)}
    factors = {'L0_gnn_b': 3.242, 'L1_gnn_Wq': 8.0, 'L1_gnn_Wk': 8.0}
    for name, (base, spread) in spreads.items():
        noise = np.random.default_rng([zlib.crc32(name.encode()), seed]).standard_normal(out[name].shape)
        drawn = base * np.exp(spread * noise) if base else spread * noise
        out[name] = jnp.asarray(drawn.astype(out[name].dtype))
    for name, factor in factors.items():
        out[name] = (out[name] * factor).astype(out[name].dtype)
    return out
```

```python
from contextlib import ExitStack

import numpy as np
import concourse.bass as bass
from concourse import mybir

ALU = mybir.AluOpType
ACT = mybir.ActivationFunctionType
F32 = mybir.dt.float32
F16 = mybir.dt.float16
U32 = mybir.dt.uint32
AX = mybir.AxisListType

P = 128
H, HD = 8, 64
GROUP = 4
RING = 8
H_SCALE = 2.0 ** 11
W_SCALE = 2.0 ** 14
EXP_BITS = 0x7F800000
NORM_AHEAD, PREP_AHEAD, ATTN_BEHIND = 6, 4, 4
LOAD_AHEAD, X1_AHEAD, OUT_BEHIND = 8, 3, 5


def graph_layers(nc, x, adj, b0, wq, bq, wk, bk, wv, bv, out):
    B, N, D = x.shape
    assert N == P and D == H * HD and B % (2 * GROUP) == 0
    KC = D // P
    VW = HD + 1

    with ExitStack() as ctx:
        def sb(name, shape, dt=F32):
            return ctx.enter_context(nc.sbuf_tensor(name, shape, dt))

        def ps(name, shape, dt=F32):
            return ctx.enter_context(nc.psum_tensor(name, shape, dt))

        def sem(name):
            return ctx.enter_context(nc.semaphore(name))

        ident = sb("ident", [P, P])
        ident16 = sb("ident16", [P, P], F16)
        ones = sb("ones", [P, P])
        adj_sb = sb("adj_sb", [P, P])
        mask8 = sb("mask8", [P, P])
        adjT = sb("adjT", [P, 2, P], F16)
        w_raw = sb("w_raw", [P, 3, KC, D])
        w16 = sb("w16", [P, 3, 2, KC, D], F16)
        bqk = sb("bqk", [P, 2, KC])
        b0_col = sb("b0_col", [P, 1])
        bv_rows = sb("bv_rows", [P, D])
        peak = sb("peak", [P, 4])
        peak_all = sb("peak_all", [P, 4])
        peak_min = sb("peak_min", [P, 4])
        pow2 = sb("pow2", [P, 4])
        pow2_inv = sb("pow2_inv", [P, 4])
        pow2_inv15 = sb("pow2_inv15", [P, 4])
        pow2_invx = sb("pow2_invx", [P, 4])
        up = sb("up", [P, 4])
        down = sb("down", [P, 4])
        minus_half = sb("minus_half", [P, 1])
        eps = sb("eps", [P, 1])
        plus_minus = sb("plus_minus", [P, 2])
        x_in = sb("x_in", [P, RING, D])
        x1 = sb("x1", [P, RING, D])
        y = sb("y", [P, 2, D])
        stats = sb("stats", [P, 2, 6])
        mean_var = sb("mean_var", [P, 2, 2])
        var_eps = sb("var_eps", [P, 2, 1])
        inv_std = sb("inv_std", [P, 2, 1])
        h_mul = sb("h_mul", [P, 2, 2])
        h_add = sb("h_add", [P, 2, 1])
        h32 = sb("h32", [P, 2, D])
        h16 = sb("h16", [P, 4, 2, D], F16)
        hT = sb("hT", [P, 2, 2, KC, GROUP, P], F16)
        a_max = sb("a_max", [P, RING, 1])
        c_col = sb("c_col", [P, RING, 1])
        qkT = sb("qkT", [P, 2, 2, KC, GROUP, P])
        v = sb("v", [P, 2, GROUP, H, VW])
        masked = sb("masked", [P, H, P])
        row_max = sb("row_max", [P, H])
        shifted = sb("shifted", [P, H, P])
        probs = sb("probs", [P, H, P])
        probsT = sb("probsT", [P, H, P])
        inv_sum = sb("inv_sum", [P, 2, H // 2])
        attn = sb("attn", [P, 2, D])
        ring = ps("ring", [P, 4, 512])
        sc = ps("sc", [P, 2, 512])
        o_ps = ps("o_ps", [P, 2, 512])
        o_view = o_ps[:, :, 0:H // 2 * VW].rearrange("p t (h e) -> p t h e", e=VW)

        x_loaded = [sem(f"x_loaded{i}") for i in range(RING)]
        y_stored = [sem(f"y_stored{i}") for i in range(2)]
        adj_loaded, w_loaded, bias_loaded = sem("adj_loaded"), sem("w_loaded"), sem("bias_loaded")
        ident_step, pool_const = sem("ident_step"), sem("pool_const")
        peak_done, peak_all_done, scale_step, scale_done = sem("peak_done"), sem("peak_all_done"), sem("scale_step"), sem("scale_done")
        mask_done, adjT_ready, heads_done, rests_done = sem("mask_done"), sem("adjT_ready"), sem("heads_done"), sem("rests_done")
        bn_done, mv_done, norm_step, norm_done = sem("bn_done"), sem("mv_done"), sem("norm_step"), sem("norm_done")
        h32_done, h_head_done, h_rest_done = sem("h32_done"), sem("h_head_done"), sem("h_rest_done")
        t_ready, t_evac = sem("t_ready"), sem("t_evac")
        a_ready, a_evac = sem("a_ready"), sem("a_evac")
        qk_ready, qk_evac = sem("qk_ready"), sem("qk_evac")
        v_ready, v_evac = sem("v_ready"), sem("v_evac")
        s_ready, masked_done, max_done, shifted_done, probs_done = (
            sem("s_ready"), sem("masked_done"), sem("max_done"), sem("shifted_done"), sem("probs_done"))
        pt_ready, pt_evac = sem("pt_ready"), sem("pt_evac")
        o_ready, inv_sum_done, o_evac = sem("o_ready"), sem("inv_sum_done"), sem("o_evac")
        c_done, x1_done, y_done = sem("c_done"), sem("x1_done"), sem("y_done")

        def wait(eng, s, count):
            if not isinstance(count, int) or count > 0:
                eng.wait_ge(s, count)

        def in_range(base, k):
            return not isinstance(base, int) or 0 <= base + k < B

        def ring_place(k, i):
            return (5 * k + i) % 4

        def slots(eng, slot):
            for k in range(RING):
                slot(0, k)
            with eng.Fori(RING, B - 2 * RING + 1, RING) as base:
                for k in range(RING):
                    slot(base, k)
            for k in range(RING):
                slot(B - RING, k)
            for k in range(GROUP + 1):
                slot(B, k)

        block = ctx.enter_context(nc.Block())

        @block.sync
        def _(sp):
            def load(base, k):
                if in_range(base, k):
                    wait(sp, x1_done, base + k - RING + 1)
                    sp.dma_start(x_in[:, k % RING, :], x[base + k, :, :]).then_inc(x_loaded[k % RING], 16)

            def store(base, k):
                if in_range(base, k):
                    sp.wait_ge(y_done, base + k + 1)
                    sp.dma_start(out[base + k, :, :], y[:, k % 2, :]).then_inc(y_stored[k % 2], 16)

            load(0, 0)
            sp.dma_start(adj_sb[:, :], adj).then_inc(adj_loaded, 16)
            load(0, 1)
            for j, w in enumerate((wq, wk, wv)):
                sp.dma_start(w_raw[:, j, :, :], w.rearrange("(c p) n -> p c n", p=P)).then_inc(w_loaded, 16)
            sp.dma_start(b0_col[:, :], b0.rearrange("(p a) -> p a", a=1)).then_inc(bias_loaded, 16)
            sp.dma_start(bqk[:, 0, :], bq.rearrange("(c p) -> p c", p=P), allow_slow_non_contiguous=True).then_inc(bias_loaded, 16)
            sp.dma_start(bqk[:, 1, :], bk.rearrange("(c p) -> p c", p=P), allow_slow_non_contiguous=True).then_inc(bias_loaded, 16)
            sp.dma_start(bv_rows[:, :], bv.partition_broadcast(P)).then_inc(bias_loaded, 16)
            for k in range(2, LOAD_AHEAD):
                load(0, k)

            def slot(base, k):
                store(base, k - OUT_BEHIND)
                load(base, k + LOAD_AHEAD)

            slots(sp, slot)
            for k in range(2):
                sp.wait_ge(y_stored[k], 16 * (B // 2))

        @block.gpsimd
        def _(pool):
            pool.memset(ident[:, :], 0.0).then_inc(ident_step, 1)
            pool.memset(minus_half[:, :], -0.5).then_inc(pool_const, 1)
            pool.memset(eps[:, :], 1e-5).then_inc(pool_const, 1)
            pool.memset(plus_minus[:, 0:1], H_SCALE).then_inc(pool_const, 1)
            pool.memset(plus_minus[:, 1:2], -H_SCALE).then_inc(pool_const, 1)
            pool.wait_ge(ident_step, 1)
            pool.affine_select(out=ident[:, :], in_=ident[:, :], compare_op=ALU.not_equal, fill=1.0, base=0,
                               pattern=[[-1, P]], channel_multiplier=1).then_inc(ident_step, 1)
            pool.wait_ge(ident_step, 2)
            pool.tensor_copy(ident16[:, :], ident[:, :]).then_inc(pool_const, 1)
            pool.wait_ge(pool_const, 4)

            def norm_scales(base, k):
                if in_range(base, k):
                    r = k % 2
                    m = base + k
                    pool.wait_ge(mv_done, m + 1)
                    pool.tensor_tensor(var_eps[:, r, :], mean_var[:, r, 1:2], eps[:, :], ALU.add).then_inc(norm_step, 1)
                    pool.wait_ge(norm_step, 3 * m + 1)
                    pool.tensor_tensor(inv_std[:, r, :], var_eps[:, r, :], minus_half[:, :],
                                       ALU.pow).then_inc(norm_step, 1)
                    pool.wait_ge(norm_step, 3 * m + 2)
                    wait(pool, h_head_done, m - 1)
                    wait(pool, h32_done, m - 1)
                    pool.tensor_tensor(h_mul[:, r, :], inv_std[:, r, :].to_broadcast([P, 2]), plus_minus[:, :],
                                       ALU.mult).then_inc(norm_step, 1)
                    pool.wait_ge(norm_step, 3 * m + 3)
                    pool.tensor_tensor(h_add[:, r, :], mean_var[:, r, 0:1], h_mul[:, r, 1:2],
                                       ALU.mult).then_inc(norm_done, 1)

            def rest(base, k):
                if in_range(base, k):
                    pool.wait_ge(h32_done, base + k + 1)
                    pool.wait_ge(h_head_done, base + k + 1)
                    wait(pool, a_ready, base + k - 3)
                    pool.tensor_tensor(h16[:, k % 4, 1, :], h32[:, k % 2, :], h16[:, k % 4, 0, :],
                                       ALU.subtract).then_inc(h_rest_done, 1)

            def finish(base, k):
                if in_range(base, k):
                    m = base + k
                    pool.wait_ge(o_evac, m + 1)
                    pool.wait_ge(x1_done, m + 1)
                    wait(pool, y_stored[k % 2], (m - k % 2) * 8)
                    pool.tensor_tensor(y[:, k % 2, :], attn[:, k % 2, :], x1[:, k % RING, :],
                                       ALU.add).then_inc(y_done, 1)

            def add_c(base, k):
                if in_range(base, k):
                    m = base + k
                    pool.wait_ge(c_done, m + 1)
                    wait(pool, y_done, m - RING + 1)
                    pool.tensor_tensor(x1[:, k % RING, :], x_in[:, k % RING, :],
                                       c_col[:, k % RING, :].to_broadcast([P, D]), ALU.add).then_inc(x1_done, 1)

            norm_scales(0, 0)
            pool.wait_ge(peak_done, 4)
            pool.partition_all_reduce(peak_all[:, :], peak[:, :], P, bass.bass_isa.ReduceOp.max).then_inc(peak_all_done, 1)
            for k in range(NORM_AHEAD):
                if k:
                    norm_scales(0, k)
                rest(0, k)
            for k in range(X1_AHEAD):
                add_c(0, k)

            def slot(base, k):
                finish(base, k - OUT_BEHIND)
                norm_scales(base, k + NORM_AHEAD)
                rest(base, k + NORM_AHEAD)
                add_c(base, k + X1_AHEAD)

            slots(pool, slot)

        @block.scalar
        def _(act):
            def normalise(base, k):
                if in_range(base, k):
                    m = base + k
                    act.wait_ge(norm_done, m + 1)
                    wait(act, h_rest_done, m - 1)
                    wait(act, a_ready, m - 3)
                    args = dict(scale=h_mul[:, k % 2, 0:1], bias=h_add[:, k % 2, :])
                    nc.scalar.activation(h32[:, k % 2, :], x_in[:, k % RING, :], ACT.Relu, **args).then_inc(h32_done, 1)
                    nc.scalar.activation(h16[:, k % 4, 0, :], x_in[:, k % RING, :], ACT.Relu, **args).then_inc(h_head_done, 1)

            def qk_out(base, k, u):
                if in_range(base, k):
                    act.wait_ge(qk_ready, 2 * (base + k) + u % 2 + 1)
                    nc.scalar.activation(qkT[:, k // GROUP % 2, u // KC, u % KC, :, :].rearrange("p g n -> p (g n)"),
                                         ring[:, ring_place(k, 1 + u % 2), :], ACT.Identity,
                                         scale=down[:, u // KC:u // KC + 1],
                                         bias=bqk[:, u // KC, u % KC:u % KC + 1]).then_inc(qk_evac, 1)

            def exps(base, k):
                if in_range(base, k):
                    m = base + k
                    act.wait_ge(shifted_done, m + 1)
                    wait(act, pt_ready, m)
                    nc.scalar.activation(probs[:, :, :], shifted[:, :, :], ACT.Exp, scale=HD ** -0.5).then_inc(probs_done, 1)

            def probs_out(base, k):
                if in_range(base, k):
                    m = base + k
                    act.wait_ge(pt_ready, m + 1)
                    wait(act, o_ready, m)
                    nc.scalar.activation(probsT[:, :, :].rearrange("p h n -> p (h n)"),
                                         sc[:, :, :].rearrange("p t n -> p (t n)"), ACT.Copy).then_inc(pt_evac, 1)

            def c_of(base, k):
                if in_range(base, k):
                    m = base + k
                    act.wait_ge(a_evac, m + 1)
                    wait(act, x1_done, m - RING + 1)
                    nc.scalar.activation(c_col[:, k % RING, :], a_max[:, k % RING, :], ACT.Relu, scale=down[:, 3:4],
                                         bias=b0_col[:, :]).then_inc(c_done, 1)

            normalise(0, 0)
            act.wait_ge(scale_done, 2)
            act.wait_ge(adjT_ready, 1)
            nc.scalar.activation(adjT[:, 0, :], ring[:, 0, 0:P], ACT.Identity, scale=up[:, 3:4]).then_inc(heads_done, 1)
            for j in range(3):
                nc.scalar.activation(w16[:, j, 0, :, :], w_raw[:, j, :, :], ACT.Identity, scale=up[:, j:j + 1]).then_inc(heads_done, 1)
            for k in range(1, NORM_AHEAD):
                normalise(0, k)
            act.wait_ge(bias_loaded, 64)
            for k in range(X1_AHEAD):
                c_of(0, k)

            def slot(base, k):
                u = 2 * (k % GROUP)
                qk_out(base, k, u)
                exps(base, k - ATTN_BEHIND)
                qk_out(base, k, u + 1)
                probs_out(base, k - ATTN_BEHIND)
                normalise(base, k + NORM_AHEAD)
                c_of(base, k + X1_AHEAD)

            slots(act, slot)

        @block.vector
        def _(dve):
            def stats_of(base, k):
                if in_range(base, k):
                    m = base + k
                    dve.wait_ge(x_loaded[k % RING], 16 * 1 + (m - k % RING) * 2)
                    nc.vector.bn_stats(stats[:, k % 2, :], x_in[:, k % RING, :]).then_inc(bn_done, 1)

            def moments_wait(base, k):
                if in_range(base, k):
                    dve.wait_ge(bn_done, base + k + 1)
                    wait(dve, norm_done, base + k - 1)

            def moments_of(base, k):
                if in_range(base, k):
                    nc.vector.bn_aggr(mean_var[:, k % 2, :], stats[:, k % 2, :]).then_inc(mv_done, 1)

            def transpose_out(base, k, place):
                if in_range(base, k):
                    m = base + k
                    dve.wait_ge(t_ready, m + 1)
                    nc.vector.tensor_copy(
                        hT[:, k // GROUP % 2, :, :, k % GROUP, :].rearrange("p s c n -> p (s c) n"),
                        ring[:, place, :].bitcast(F16).rearrange("p (s n) -> p s n", n=P)).then_inc(t_evac, 1)

            def adjacency_out(base, k, place):
                if in_range(base, k):
                    m = base + k
                    dve.wait_ge(a_ready, m + 1)
                    wait(dve, c_done, m - RING + 1)
                    nc.vector.tensor_reduce(a_max[:, k % RING, :], ring[:, place, :], AX.X, ALU.max).then_inc(a_evac, 1)

            def v_out(base, k, place):
                if in_range(base, k):
                    dve.wait_ge(v_ready, base + k + 1)
                    nc.vector.scalar_tensor_tensor(
                        v[:, k // GROUP % 2, k % GROUP, :, 0:HD],
                        ring[:, place, :].rearrange("p (h d) -> p h d", d=HD), down[:, 2:3],
                        bv_rows[:, :].rearrange("p (h d) -> p h d", d=HD), ALU.mult, ALU.add).then_inc(v_evac, 1)

            def softmax_shift(base, k):
                if in_range(base, k):
                    m = base + k
                    dve.wait_ge(s_ready, m + 1)
                    nc.vector.tensor_tensor(masked[:, :, :], sc[:, :, :].rearrange("p t (h n) -> p (t h) n", n=P),
                                            mask8[:, :].unsqueeze(1).to_broadcast([P, H, P]), ALU.add).then_inc(masked_done, 1)
                    dve.wait_ge(masked_done, m + 1)
                    nc.vector.tensor_reduce(row_max[:, :], masked[:, :, :], AX.X, ALU.max).then_inc(max_done, 1)
                    dve.wait_ge(max_done, m + 1)
                    wait(dve, probs_done, m)
                    nc.vector.tensor_tensor(shifted[:, :, :], masked[:, :, :],
                                            row_max[:, :].unsqueeze(2).to_broadcast([P, H, P]), ALU.subtract).then_inc(shifted_done, 1)

            def attention_out(base, k):
                if in_range(base, k):
                    m = base + k
                    dve.wait_ge(o_ready, m + 1)
                    nc.vector.reciprocal(inv_sum[:, :, :], o_view[:, :, :, HD]).then_inc(inv_sum_done, 1)
                    dve.wait_ge(inv_sum_done, m + 1)
                    wait(dve, y_done, m - 1)
                    nc.vector.tensor_tensor(attn[:, k % 2, :].rearrange("p (t h d) -> p t h d", t=2, d=HD),
                                            o_view[:, :, :, 0:HD],
                                            inv_sum[:, :, :].unsqueeze(3).to_broadcast([P, 2, H // 2, HD]),
                                            ALU.mult).then_inc(o_evac, 1)

            stats_of(0, 0)
            moments_wait(0, 0)
            moments_of(0, 0)
            dve.wait_ge(adj_loaded, 16)
            nc.vector.tensor_reduce(peak[:, 3:4], adj_sb[:, :], AX.X, ALU.max, apply_absolute_value=True).then_inc(peak_done, 1)
            nc.vector.tensor_scalar(mask8[:, :], adj_sb[:, :], 0.0, -8e9, ALU.is_equal, ALU.mult).then_inc(mask_done, 1)
            nc.vector.memset(v[:, :, :, :, HD:VW].rearrange("p a g h e -> p (a g h) e"), 1.0).then_inc(mask_done, 1)
            dve.wait_ge(w_loaded, 48)
            for j in range(3):
                nc.vector.tensor_reduce(peak[:, j:j + 1], w_raw[:, j, :, :].rearrange("p c n -> p (c n)"), AX.X, ALU.max,
                                        apply_absolute_value=True).then_inc(peak_done, 1)
            dve.wait_ge(peak_all_done, 1)
            nc.vector.tensor_scalar(peak_min[:, :], peak_all[:, :], 2.0 ** -100, None, ALU.max).then_inc(scale_step, 1)
            dve.wait_ge(scale_step, 1)
            nc.vector.tensor_scalar(pow2[:, :].bitcast(U32), peak_min[:, :].bitcast(U32), EXP_BITS, None,
                                    ALU.bitwise_and).then_inc(scale_step, 1)
            dve.wait_ge(scale_step, 2)
            nc.vector.reciprocal(pow2_inv[:, :], pow2[:, :]).then_inc(scale_step, 1)
            dve.wait_ge(scale_step, 3)
            nc.vector.tensor_scalar(pow2_inv15[:, :], pow2_inv[:, :], 1.5, None, ALU.mult).then_inc(scale_step, 1)
            dve.wait_ge(scale_step, 4)
            nc.vector.tensor_scalar(pow2_invx[:, :].bitcast(U32), pow2_inv15[:, :].bitcast(U32), EXP_BITS, None,
                                    ALU.bitwise_and).then_inc(scale_step, 1)
            dve.wait_ge(scale_step, 5)
            nc.vector.tensor_scalar(up[:, :], pow2_invx[:, :], W_SCALE, None, ALU.mult).then_inc(scale_done, 1)
            nc.vector.tensor_scalar(down[:, :], pow2[:, :], 1.0 / (W_SCALE * H_SCALE), None, ALU.mult).then_inc(scale_done, 1)
            dve.wait_ge(scale_done, 2)
            dve.wait_ge(heads_done, 1)
            nc.vector.scalar_tensor_tensor(adjT[:, 1, :], ring[:, 0, 0:P], up[:, 3:4], adjT[:, 0, :],
                                           ALU.mult, ALU.subtract).then_inc(rests_done, 1)
            for k in range(1, GROUP):
                stats_of(0, k)
                moments_wait(0, k)
                moments_of(0, k)
            for j in range(3):
                dve.wait_ge(heads_done, j + 2)
                nc.vector.scalar_tensor_tensor(w16[:, j, 1, :, :].rearrange("p c n -> p (c n)"),
                                               w_raw[:, j, :, :].rearrange("p c n -> p (c n)"), up[:, j:j + 1],
                                               w16[:, j, 0, :, :].rearrange("p c n -> p (c n)"),
                                               ALU.mult, ALU.subtract).then_inc(rests_done, 1)
            for k in range(GROUP, NORM_AHEAD):
                stats_of(0, k)
                moments_wait(0, k)
                moments_of(0, k)
            for k in range(PREP_AHEAD):
                transpose_out(0, k, 2 * k % 4)
                adjacency_out(0, k, (2 * k + 1) % 4)
            dve.wait_ge(bias_loaded, 64)
            dve.wait_ge(mask_done, 2)

            def slot(base, k):
                transpose_out(base, k + PREP_AHEAD, ring_place(k, 0))
                softmax_shift(base, k - ATTN_BEHIND)
                attention_out(base, k - OUT_BEHIND)
                stats_of(base, k + NORM_AHEAD)
                moments_wait(base, k + NORM_AHEAD)
                adjacency_out(base, k + PREP_AHEAD, ring_place(k, 3))
                moments_of(base, k + NORM_AHEAD)
                v_out(base, k, ring_place(k, 4))

            slots(dve, slot)

        @block.tensor
        def _(pe):
            PAIRS = ((0, 0), (0, 1), (1, 0))

            def transposes(base, k, place):
                if in_range(base, k):
                    pe.wait_ge(h_rest_done, base + k + 1)
                    t = ring[:, place, :].bitcast(F16)
                    for s in range(2):
                        for c in range(KC):
                            i = s * KC + c
                            last = nc.tensor.transpose(t[:, i * P:(i + 1) * P], h16[:, k % 4, s, c * P:(c + 1) * P], ident16[:, :])
                    last.then_inc(t_ready, 1)

            def adjacency(base, k, place):
                if in_range(base, k):
                    for i, (s, t) in enumerate(PAIRS):
                        last = nc.tensor.matmul(ring[:, place, :], adjT[:, s, :], h16[:, k % 4, t, :],
                                                start=(i == 0), stop=(i == 2))
                    last.then_inc(a_ready, 1)

            def qk_chunk(base, k, u, place):
                if in_range(base, k):
                    j, col = u // KC, u % KC
                    for c in range(KC):
                        for i, (s, t) in enumerate(PAIRS):
                            last = nc.tensor.matmul(ring[:, place, :], w16[:, j, s, c, col * P:(col + 1) * P],
                                                    hT[:, k // GROUP % 2, t, c, :, :].rearrange("p g n -> p (g n)"),
                                                    start=(c == 0 and i == 0), stop=(c == KC - 1 and i == 2))
                    last.then_inc(qk_ready, 1)

            def v_rows(base, k, place):
                if in_range(base, k):
                    for c in range(KC):
                        for i, (s, t) in enumerate(PAIRS):
                            last = nc.tensor.matmul(ring[:, place, :], hT[:, k // GROUP % 2, s, c, k % GROUP, :],
                                                    w16[:, 2, t, c, :], start=(c == 0 and i == 0),
                                                    stop=(c == KC - 1 and i == 2))
                    last.then_inc(v_ready, 1)

            def scores(base, k, groups_done):
                if in_range(base, k):
                    m = base + k
                    pe.wait_ge(qk_evac, groups_done)
                    wait(pe, pt_evac, m)
                    for h in range(H):
                        lo, c = h % 2 * HD, h // 2
                        q = qkT[lo:lo + HD, k // GROUP % 2, 0, c, k % GROUP, :]
                        kk = qkT[lo:lo + HD, k // GROUP % 2, 1, c, k % GROUP, :]
                        last = nc.tensor.matmul(sc[:, h % 2, c * P:(c + 1) * P], q, kk, start=True, stop=True)
                        if h == H - 2:
                            last_even = last
                    last.then_inc(s_ready, 1)

            def probs_transposed(base, k):
                if in_range(base, k):
                    pe.wait_ge(probs_done, base + k + 1)
                    for i in range(H):
                        last = nc.tensor.transpose(sc[:, i // 4, i % 4 * P:(i % 4 + 1) * P], probs[:, i, :], ident[:, :])
                    last.then_inc(pt_ready, 1)

            def probs_times_v(base, k):
                if in_range(base, k):
                    m = base + k
                    pe.wait_ge(pt_evac, m + 1)
                    pe.wait_ge(v_evac, m + 1)
                    wait(pe, o_evac, m)
                    for h in range(H):
                        last = nc.tensor.matmul(o_view[:, h // 4, h % 4, :], probsT[:, h % 2 * 4 + h // 2, :],
                                                v[:, k // GROUP % 2, k % GROUP, h, :], start=True, stop=True)
                    last.then_inc(o_ready, 1)

            pe.wait_ge(ident_step, 2)
            pe.wait_ge(adj_loaded, 16)
            nc.tensor.transpose(ring[:, 0, 0:P], adj_sb[:, :], ident[:, :]).then_inc(adjT_ready, 1)
            pe.wait_ge(rests_done, 1)
            pe.wait_ge(pool_const, 5)
            for k in range(PREP_AHEAD):
                if k >= 2:
                    pe.wait_ge(t_evac, k - 1)
                    pe.wait_ge(a_evac, k - 1)
                transposes(0, k, 2 * k % 4)
                adjacency(0, k, (2 * k + 1) % 4)
            pe.wait_ge(rests_done, 4)

            def slot(base, k):
                n = base + k
                u = 2 * (k % GROUP)
                if isinstance(base, int) and n == 0:
                    pe.wait_ge(t_evac, PREP_AHEAD)
                    pe.wait_ge(a_evac, PREP_AHEAD)
                if in_range(base, k + PREP_AHEAD):
                    wait(pe, qk_evac, 2 * n - 1)
                transposes(base, k + PREP_AHEAD, ring_place(k, 0))
                scores(base, k - ATTN_BEHIND, 2 * (n - k % GROUP))
                if in_range(base, k):
                    if k % GROUP == 0:
                        pe.wait_ge(t_evac, n + GROUP)
                    wait(pe, qk_evac, 2 * n)
                qk_chunk(base, k, u, ring_place(k, 1))
                if in_range(base, k):
                    pe.wait_ge(a_evac, n + PREP_AHEAD if not isinstance(base, int) else min(n + PREP_AHEAD, B))
                qk_chunk(base, k, u + 1, ring_place(k, 2))
                probs_transposed(base, k - ATTN_BEHIND)
                if in_range(base, k + PREP_AHEAD):
                    wait(pe, v_evac, n)
                adjacency(base, k + PREP_AHEAD, ring_place(k, 3))
                if in_range(base, k):
                    wait(pe, t_evac, n + PREP_AHEAD + 1 if not isinstance(base, int) else min(n + PREP_AHEAD + 1, B))
                    wait(pe, qk_evac, 2 * n - 1)
                v_rows(base, k, ring_place(k, 4))
                probs_times_v(base, k - ATTN_BEHIND)

            slots(pe, slot)


_INS = ["x", "adj", "L0_gnn_b", "L1_gnn_Wq", "L1_gnn_bq", "L1_gnn_Wk", "L1_gnn_bk", "L1_gnn_Wv", "L1_gnn_bv"]


def kernel(**inputs):
    import concourse.bacc as _bacc
    from concourse.bass_utils import run_bass_kernel_spmd as _run

    nc = _bacc.Bacc("TRN2", target_bir_lowering=False, num_devices=1)
    arrays, args = {}, []
    for name in _INS:
        a = np.ascontiguousarray(inputs[name])
        arrays[f"in_{name}"] = a
        args.append(nc.dram_tensor(f"in_{name}", a.shape, mybir.dt.from_np(a.dtype), kind="ExternalInput").ap())
    out = nc.dram_tensor("out_x", inputs["x"].shape, F32, kind="ExternalOutput").ap()
    graph_layers(nc, *args, out)
    r = _run(nc, [arrays], core_ids=[0])
    return r.results[0]["out_x"]
```

```python
from contextlib import ExitStack

import numpy as np
import concourse.bass as bass
from concourse import mybir

ALU = mybir.AluOpType
ACT = mybir.ActivationFunctionType
F32 = mybir.dt.float32
F16 = mybir.dt.float16
U32 = mybir.dt.uint32
AX = mybir.AxisListType

P = 128
H, HD = 8, 64
GROUP = 4
RING = 8
H_SCALE = 2.0 ** 11
W_SCALE = 2.0 ** 14
P_SCALE = 2.0 ** -21
BIAS_SHARE = 2.0 ** -8
EXP_BITS = 0x7F800000
LOAD_AHEAD, MOMENTS_AHEAD, NORM_AHEAD, PREP_AHEAD, X1_AHEAD = 8, 6, 5, 4, 1
ATTN_BEHIND, OUT_BEHIND = 5, 6


def graph_layers(nc, x, adj, b0, wq, bq, wk, bk, wv, bv, out):
    B, N, D = x.shape
    assert N == P and D == H * HD and B % (2 * GROUP) == 0
    KC = D // P
    VW = HD + 1
    VP = HD + 2

    with ExitStack() as ctx:
        def sb(name, shape, dt=F32):
            return ctx.enter_context(nc.sbuf_tensor(name, shape, dt))

        def ps(name, shape, dt=F32):
            return ctx.enter_context(nc.psum_tensor(name, shape, dt))

        def sem(name):
            return ctx.enter_context(nc.semaphore(name))

        ident = sb("ident", [P, P])
        ident16 = sb("ident16", [P, P], F16)
        ones = sb("ones", [P, P])
        adj_sb = sb("adj_sb", [P, P])
        mask8 = sb("mask8", [P, P])
        adjT = sb("adjT", [P, 2, P], F16)
        w_raw = sb("w_raw", [P, 3, KC, D])
        w16 = sb("w16", [P, 3, 2, KC, D], F16)
        bqk = sb("bqk", [P, 2, KC])
        b0_col = sb("b0_col", [P, 1])
        bv_rows = sb("bv_rows", [P, D])
        peak = sb("peak", [P, 4])
        peak_all = sb("peak_all", [P, 4])
        peak_min = sb("peak_min", [P, 4])
        pow2 = sb("pow2", [P, 4])
        pow2_inv = sb("pow2_inv", [P, 4])
        pow2_inv15 = sb("pow2_inv15", [P, 4])
        pow2_invx = sb("pow2_invx", [P, 4])
        up = sb("up", [P, 4])
        down = sb("down", [P, 4])
        undo = sb("undo", [P, 3])
        redo = sb("redo", [P, 2])
        score_scale = sb("score_scale", [P, 1])
        bqk_peak = sb("bqk_peak", [P, 2])
        w_peak = sb("w_peak", [P, 2])
        bqk_up = sb("bqk_up", [P, 2, KC])
        minus_half = sb("minus_half", [P, 1])
        eps = sb("eps", [P, 1])
        plus_minus = sb("plus_minus", [P, 2])
        x_in = sb("x_in", [P, RING, D])
        xbv = sb("xbv", [P, D])
        x1 = sb("x1", [P, RING, D])
        y = sb("y", [P, 2, D])
        stats = sb("stats", [P, 2, 6])
        mean_var = sb("mean_var", [P, 2, 2])
        var_eps = sb("var_eps", [P, 2, 1])
        inv_std = sb("inv_std", [P, 2, 1])
        h_mul = sb("h_mul", [P, 2, 2])
        h_add = sb("h_add", [P, 2, 1])
        h32 = sb("h32", [P, 2, D])
        h16 = sb("h16", [P, 4, 2, D], F16)
        hT = sb("hT", [P, 2, 2, KC, GROUP, P], F16)
        a_max = sb("a_max", [P, RING, 1])
        c_col = sb("c_col", [P, RING, 1])
        qk32 = sb("qk32", [P, 2, GROUP * P])
        qkT = sb("qkT", [P, 2, 2, 2, KC, GROUP, P], F16)
        v16 = sb("v16", [P, 2, 2, GROUP, H, VP], F16)
        masked = sb("masked", [P, H, P])
        row_max = sb("row_max", [P, H])
        shifted = sb("shifted", [P, H, P])
        probs = sb("probs", [P, H, P])
        probsT = sb("probsT", [P, 2, H, P], F16)
        inv_sum = sb("inv_sum", [P, 2, H // 2])
        out_scale = sb("out_scale", [P, 2, H // 2])
        attn = sb("attn", [P, 2, D])
        ring = ps("ring", [P, 4, 512])
        sc = ps("sc", [P, 2, 512])
        o_ps = ps("o_ps", [P, 2, 512])
        o_view = o_ps[:, :, 0:H // 2 * VW].rearrange("p t (h e) -> p t h e", e=VW)

        x_loaded = [sem(f"x_loaded{i}") for i in range(RING)]
        y_stored = [sem(f"y_stored{i}") for i in range(2)]
        adj_loaded, w_loaded, bias_loaded = sem("adj_loaded"), sem("w_loaded"), sem("bias_loaded")
        ident_step, pool_const = sem("ident_step"), sem("pool_const")
        peak_done, peak_all_done, scale_step, scale_done = sem("peak_done"), sem("peak_all_done"), sem("scale_step"), sem("scale_done")
        mask_done, adjT_ready, heads_done, rests_done = sem("mask_done"), sem("adjT_ready"), sem("heads_done"), sem("rests_done")
        bn_done, mv_done, norm_step, norm_done = sem("bn_done"), sem("mv_done"), sem("norm_step"), sem("norm_done")
        h32_done, h_head_done, h_rest_done = sem("h32_done"), sem("h_head_done"), sem("h_rest_done")
        t_ready, t_evac = sem("t_ready"), sem("t_evac")
        a_ready, a_evac = sem("a_ready"), sem("a_evac")
        qk_ready, qk_evac, qk_head_done, qk_rest_done = sem("qk_ready"), sem("qk_evac"), sem("qk_head_done"), sem("qk_rest_done")
        v_ready, v_head_done, v_evac = sem("v_ready"), sem("v_head_done"), sem("v_evac")
        s_ready, masked_done, max_done, shifted_done, probs_done = (
            sem("s_ready"), sem("masked_done"), sem("max_done"), sem("shifted_done"), sem("probs_done"))
        pt_ready, pt_head_done, pt_evac = sem("pt_ready"), sem("pt_head_done"), sem("pt_evac")
        o_ready, inv_sum_done, out_scale_done, o_evac = sem("o_ready"), sem("inv_sum_done"), sem("out_scale_done"), sem("o_evac")
        c_done, xc_done, x1_done, y_done = sem("c_done"), sem("xc_done"), sem("x1_done"), sem("y_done")

        def wait(eng, s, count):
            if not isinstance(count, int) or count > 0:
                eng.wait_ge(s, count)

        def in_range(base, k):
            return not isinstance(base, int) or 0 <= base + k < B

        def ring_place(k, i):
            return (5 * k + i) % 4

        def qk_place(k, u, part):
            return qkT[:, k // GROUP % 2, part, u // KC, u % KC, :, :].rearrange("p g n -> p (g n)")

        TAIL = [(B, k) for k in range(-ATTN_BEHIND, 0)]
        pairs_of_banks = (sc, ring)

        def slots(eng, slot):
            for k in range(RING):
                slot(0, k)
            with eng.Fori(RING, B - 2 * RING + 1, RING) as base:
                for k in range(RING):
                    slot(base, k)
            for k in range(RING):
                slot(B - RING, k)

        block = ctx.enter_context(nc.Block())

        @block.sync
        def _(sp):
            def load(base, k):
                if in_range(base, k):
                    wait(sp, x1_done, base + k - RING + 1)
                    sp.dma_start(x_in[:, k % RING, :], x[base + k, :, :]).then_inc(x_loaded[k % RING], 16)

            def store(base, k):
                if in_range(base, k):
                    sp.wait_ge(y_done, base + k + 1)
                    sp.dma_start(out[base + k, :, :], y[:, k % 2, :]).then_inc(y_stored[k % 2], 16)

            load(0, 0)
            sp.dma_start(adj_sb[:, :], adj).then_inc(adj_loaded, 16)
            load(0, 1)
            for j, w in enumerate((wq, wk, wv)):
                sp.dma_start(w_raw[:, j, :, :], w.rearrange("(c p) n -> p c n", p=P)).then_inc(w_loaded, 16)
            sp.dma_start(b0_col[:, :], b0.rearrange("(p a) -> p a", a=1)).then_inc(bias_loaded, 16)
            sp.dma_start(bqk[:, 0, :], bq.rearrange("(c p) -> p c", p=P), allow_slow_non_contiguous=True).then_inc(bias_loaded, 16)
            sp.dma_start(bqk[:, 1, :], bk.rearrange("(c p) -> p c", p=P), allow_slow_non_contiguous=True).then_inc(bias_loaded, 16)
            sp.dma_start(bv_rows[:, :], bv.partition_broadcast(P)).then_inc(bias_loaded, 16)
            for k in range(2, LOAD_AHEAD):
                load(0, k)

            def slot(base, k):
                store(base, k - OUT_BEHIND)
                load(base, k + LOAD_AHEAD)

            slots(sp, slot)
            for k in range(-OUT_BEHIND, 0):
                store(B, k)
            for k in range(2):
                sp.wait_ge(y_stored[k], 16 * (B // 2))

        @block.gpsimd
        def _(pool):
            pool.memset(ident[:, :], 0.0).then_inc(ident_step, 1)
            pool.memset(minus_half[:, :], -0.5).then_inc(pool_const, 1)
            pool.memset(eps[:, :], 1e-5).then_inc(pool_const, 1)
            pool.memset(plus_minus[:, 0:1], H_SCALE).then_inc(pool_const, 1)
            pool.memset(plus_minus[:, 1:2], -H_SCALE).then_inc(pool_const, 1)
            pool.wait_ge(ident_step, 1)
            pool.affine_select(out=ident[:, :], in_=ident[:, :], compare_op=ALU.not_equal, fill=1.0, base=0,
                               pattern=[[-1, P]], channel_multiplier=1).then_inc(ident_step, 1)
            pool.wait_ge(ident_step, 2)
            pool.tensor_copy(ident16[:, :], ident[:, :]).then_inc(pool_const, 1)
            pool.wait_ge(pool_const, 4)

            def norm_scales(base, k):
                if in_range(base, k):
                    r = k % 2
                    m = base + k
                    pool.wait_ge(mv_done, m + 1)
                    pool.tensor_tensor(var_eps[:, r, :], mean_var[:, r, 1:2], eps[:, :], ALU.add).then_inc(norm_step, 1)
                    pool.wait_ge(norm_step, 3 * m + 1)
                    pool.tensor_tensor(inv_std[:, r, :], var_eps[:, r, :], minus_half[:, :],
                                       ALU.pow).then_inc(norm_step, 1)
                    pool.wait_ge(norm_step, 3 * m + 2)
                    wait(pool, h_head_done, m - 1)
                    wait(pool, h32_done, m - 1)
                    pool.tensor_tensor(h_mul[:, r, :], inv_std[:, r, :].to_broadcast([P, 2]), plus_minus[:, :],
                                       ALU.mult).then_inc(norm_step, 1)
                    pool.wait_ge(norm_step, 3 * m + 3)
                    pool.tensor_tensor(h_add[:, r, :], mean_var[:, r, 0:1], h_mul[:, r, 1:2],
                                       ALU.mult).then_inc(norm_done, 1)

            def rest(base, k):
                if in_range(base, k):
                    pool.wait_ge(h32_done, base + k + 1)
                    pool.wait_ge(h_head_done, base + k + 1)
                    wait(pool, a_ready, base + k - 3)
                    pool.tensor_tensor(h16[:, k % 4, 1, :], h32[:, k % 2, :], h16[:, k % 4, 0, :],
                                       ALU.subtract).then_inc(h_rest_done, 1)

            def finish(base, k):
                if in_range(base, k):
                    m = base + k
                    pool.wait_ge(o_evac, m + 1)
                    pool.wait_ge(x1_done, m + 1)
                    wait(pool, y_stored[k % 2], (m - k % 2) * 8)
                    pool.tensor_tensor(y[:, k % 2, :], attn[:, k % 2, :], x1[:, k % RING, :],
                                       ALU.add).then_inc(y_done, 1)

            def add_c(base, k):
                if in_range(base, k):
                    m = base + k
                    wait(pool, y_done, m - RING + 1)
                    wait(pool, x1_done, m)
                    pool.tensor_tensor(xbv[:, :], x_in[:, k % RING, :], bv_rows[:, :], ALU.add).then_inc(xc_done, 1)
                    pool.wait_ge(xc_done, m + 1)
                    pool.wait_ge(c_done, m + 1)
                    pool.tensor_tensor(x1[:, k % RING, :], xbv[:, :],
                                       c_col[:, k % RING, :].to_broadcast([P, D]), ALU.add).then_inc(x1_done, 1)

            def qk_rest(base, k, u):
                if in_range(base, k):
                    count = 2 * (base + k) + u % 2 + 1
                    pool.wait_ge(qk_evac, count)
                    pool.wait_ge(qk_head_done, count)
                    pool.tensor_tensor(qk_place(k, u, 1), qk32[:, u % 2, :], qk_place(k, u, 0),
                                       ALU.subtract).then_inc(qk_rest_done, 1)

            norm_scales(0, 0)
            pool.wait_ge(peak_done, 6)
            pool.partition_all_reduce(peak_all[:, :], peak[:, :], P, bass.bass_isa.ReduceOp.max).then_inc(peak_all_done, 1)
            for k in range(MOMENTS_AHEAD):
                if k:
                    norm_scales(0, k)
                if k < NORM_AHEAD:
                    rest(0, k)
            pool.wait_ge(bias_loaded, 64)
            for k in range(X1_AHEAD):
                add_c(0, k)

            def slot(base, k):
                u = 2 * (k % GROUP)
                add_c(base, k + X1_AHEAD)
                rest(base, k + NORM_AHEAD)
                qk_rest(base, k, u)
                finish(base, k - OUT_BEHIND)
                norm_scales(base, k + MOMENTS_AHEAD)
                qk_rest(base, k, u + 1)

            slots(pool, slot)
            for k in range(-OUT_BEHIND, 0):
                finish(B, k)

        @block.scalar
        def _(act):
            def normalise(base, k):
                if in_range(base, k):
                    m = base + k
                    act.wait_ge(norm_done, m + 1)
                    wait(act, h_rest_done, m - 1)
                    wait(act, a_ready, m - 3)
                    args = dict(scale=h_mul[:, k % 2, 0:1], bias=h_add[:, k % 2, :])
                    nc.scalar.activation(h32[:, k % 2, :], x_in[:, k % RING, :], ACT.Relu, **args).then_inc(h32_done, 1)
                    nc.scalar.activation(h16[:, k % 4, 0, :], x_in[:, k % RING, :], ACT.Relu, **args).then_inc(h_head_done, 1)

            def qk_out(base, k, u):
                if in_range(base, k):
                    count = 2 * (base + k) + u % 2 + 1
                    act.wait_ge(qk_ready, count)
                    place = ring[:, ring_place(k, 1 + u % 2), :]
                    bias = bqk_up[:, u // KC, u % KC:u % KC + 1]
                    nc.scalar.activation(qk_place(k, u, 0), place, ACT.Identity, scale=P_SCALE, bias=bias).then_inc(qk_head_done, 1)
                    wait(act, qk_rest_done, count - 2)
                    nc.scalar.activation(qk32[:, u % 2, :], place, ACT.Identity, scale=P_SCALE, bias=bias).then_inc(qk_evac, 1)

            def v_head(base, k):
                if in_range(base, k):
                    act.wait_ge(v_ready, base + k + 1)
                    nc.scalar.activation(v16[:, 0, k // GROUP % 2, k % GROUP, :, 0:HD],
                                         ring[:, ring_place(k, 4), :].rearrange("p (h d) -> p h d", d=HD),
                                         ACT.Copy, scale=P_SCALE).then_inc(v_head_done, 1)

            def exps(base, k):
                if in_range(base, k):
                    m = base + k
                    act.wait_ge(shifted_done, m + 1)
                    wait(act, pt_ready, m)
                    nc.scalar.activation(probs[:, :, :], shifted[:, :, :], ACT.Exp, scale=HD ** -0.5).then_inc(probs_done, 1)

            def probs_head(base, k, banks=sc):
                if in_range(base, k):
                    m = base + k
                    act.wait_ge(pt_ready, m + 1)
                    wait(act, o_ready, m)
                    nc.scalar.activation(probsT[:, 0, :, :].rearrange("p h n -> p (h n)"),
                                         banks[:, 0:2, :].rearrange("p t n -> p (t n)"), ACT.Copy).then_inc(pt_head_done, 1)

            def c_of(base, k):
                if in_range(base, k):
                    m = base + k
                    act.wait_ge(a_evac, m + 1)
                    wait(act, x1_done, m - RING + 1)
                    nc.scalar.activation(c_col[:, k % RING, :], a_max[:, k % RING, :], ACT.Relu, scale=down[:, 3:4],
                                         bias=b0_col[:, :]).then_inc(c_done, 1)

            normalise(0, 0)
            act.wait_ge(scale_done, 2)
            act.wait_ge(adjT_ready, 1)
            nc.scalar.activation(adjT[:, 0, :], ring[:, 0, 0:P], ACT.Identity, scale=up[:, 3:4]).then_inc(heads_done, 1)
            for j in range(3):
                nc.scalar.activation(w16[:, j, 0, :, :], w_raw[:, j, :, :], ACT.Identity, scale=up[:, j:j + 1]).then_inc(heads_done, 1)
            for k in range(1, NORM_AHEAD):
                normalise(0, k)
            act.wait_ge(bias_loaded, 64)
            act.wait_ge(scale_done, 6)
            for k in range(X1_AHEAD):
                c_of(0, k)

            def slot(base, k):
                u = 2 * (k % GROUP)
                v_head(base, k - 1)
                c_of(base, k + X1_AHEAD)
                normalise(base, k + NORM_AHEAD)
                qk_out(base, k, u)
                exps(base, k - ATTN_BEHIND)
                qk_out(base, k, u + 1)
                probs_head(base, k - ATTN_BEHIND)

            slots(act, slot)
            v_head(B, -1)
            exps(*TAIL[0])
            for i, graph in enumerate(TAIL):
                probs_head(*graph, pairs_of_banks[i % 2])
                if i + 1 < len(TAIL):
                    exps(*TAIL[i + 1])

        @block.vector
        def _(dve):
            def stats_of(base, k):
                if in_range(base, k):
                    m = base + k
                    dve.wait_ge(x_loaded[k % RING], 16 * 1 + (m - k % RING) * 2)
                    nc.vector.bn_stats(stats[:, k % 2, :], x_in[:, k % RING, :]).then_inc(bn_done, 1)

            def moments_wait(base, k):
                if in_range(base, k):
                    dve.wait_ge(bn_done, base + k + 1)
                    wait(dve, norm_done, base + k - 1)

            def moments_of(base, k):
                if in_range(base, k):
                    nc.vector.bn_aggr(mean_var[:, k % 2, :], stats[:, k % 2, :]).then_inc(mv_done, 1)

            def transpose_out(base, k, place):
                if in_range(base, k):
                    m = base + k
                    dve.wait_ge(t_ready, m + 1)
                    nc.vector.tensor_copy(
                        hT[:, k // GROUP % 2, :, :, k % GROUP, :].rearrange("p s c n -> p (s c) n"),
                        ring[:, place, :].bitcast(F16).rearrange("p (s n) -> p s n", n=P)).then_inc(t_evac, 1)

            def adjacency_out(base, k, place):
                if in_range(base, k):
                    m = base + k
                    dve.wait_ge(a_ready, m + 1)
                    wait(dve, c_done, m - RING + 1)
                    nc.vector.tensor_reduce(a_max[:, k % RING, :], ring[:, place, :], AX.X, ALU.max).then_inc(a_evac, 1)

            def v_rest(base, k):
                if in_range(base, k):
                    dve.wait_ge(v_head_done, base + k + 1)
                    nc.vector.scalar_tensor_tensor(
                        v16[:, 1, k // GROUP % 2, k % GROUP, :, 0:HD],
                        ring[:, ring_place(k, 4), :].rearrange("p (h d) -> p h d", d=HD), P_SCALE,
                        v16[:, 0, k // GROUP % 2, k % GROUP, :, 0:HD], ALU.mult, ALU.subtract).then_inc(v_evac, 1)

            def probs_rest(base, k, banks=sc):
                if in_range(base, k):
                    dve.wait_ge(pt_head_done, base + k + 1)
                    nc.vector.tensor_tensor(probsT[:, 1, :, :].rearrange("p h n -> p (h n)"),
                                            banks[:, 0:2, :].rearrange("p t n -> p (t n)"),
                                            probsT[:, 0, :, :].rearrange("p h n -> p (h n)"), ALU.subtract).then_inc(pt_evac, 1)

            def softmax_shift(base, k, banks=sc):
                if in_range(base, k):
                    m = base + k
                    wait(dve, shifted_done, m)
                    dve.wait_ge(s_ready, m + 1)
                    nc.vector.scalar_tensor_tensor(masked[:, :, :], banks[:, 0:2, :].rearrange("p t (h n) -> p (t h) n", n=P),
                                                   score_scale[:, :], mask8[:, :].unsqueeze(1).to_broadcast([P, H, P]),
                                                   ALU.mult, ALU.add).then_inc(masked_done, 1)
                    dve.wait_ge(masked_done, m + 1)
                    nc.vector.tensor_reduce(row_max[:, :], masked[:, :, :], AX.X, ALU.max).then_inc(max_done, 1)
                    dve.wait_ge(max_done, m + 1)
                    wait(dve, probs_done, m)
                    nc.vector.tensor_tensor(shifted[:, :, :], masked[:, :, :],
                                            row_max[:, :].unsqueeze(2).to_broadcast([P, H, P]), ALU.subtract).then_inc(shifted_done, 1)

            def attention_out(base, k):
                if in_range(base, k):
                    m = base + k
                    dve.wait_ge(o_ready, m + 1)
                    nc.vector.reciprocal(inv_sum[:, :, :], o_view[:, :, :, HD]).then_inc(inv_sum_done, 1)
                    dve.wait_ge(inv_sum_done, m + 1)
                    nc.vector.tensor_scalar(out_scale[:, :, :], inv_sum[:, :, :], undo[:, 2:3], None,
                                            ALU.mult).then_inc(out_scale_done, 1)
                    dve.wait_ge(out_scale_done, m + 1)
                    wait(dve, y_done, m - 1)
                    nc.vector.tensor_tensor(attn[:, k % 2, :].rearrange("p (t h d) -> p t h d", t=2, d=HD),
                                            o_view[:, :, :, 0:HD],
                                            out_scale[:, :, :].unsqueeze(3).to_broadcast([P, 2, H // 2, HD]),
                                            ALU.mult).then_inc(o_evac, 1)

            stats_of(0, 0)
            moments_wait(0, 0)
            moments_of(0, 0)
            dve.wait_ge(adj_loaded, 16)
            nc.vector.tensor_reduce(peak[:, 3:4], adj_sb[:, :], AX.X, ALU.max, apply_absolute_value=True).then_inc(peak_done, 1)
            nc.vector.tensor_scalar(mask8[:, :], adj_sb[:, :], 0.0, -8e9, ALU.is_equal, ALU.mult).then_inc(mask_done, 1)
            nc.vector.memset(v16[:, 0, :, :, :, HD:VW].rearrange("p a g h e -> p (a g h) e"), 1.0).then_inc(mask_done, 1)
            dve.wait_ge(w_loaded, 48)
            for j in range(3):
                nc.vector.tensor_reduce(w_peak[:, j:j + 1] if j < 2 else peak[:, 2:3],
                                        w_raw[:, j, :, :].rearrange("p c n -> p (c n)"), AX.X, ALU.max,
                                        apply_absolute_value=True).then_inc(peak_done, 1)
            dve.wait_ge(bias_loaded, 64)
            nc.vector.tensor_reduce(bqk_peak[:, :], bqk[:, :, :], AX.X, ALU.max, apply_absolute_value=True).then_inc(peak_done, 1)
            dve.wait_ge(peak_done, 5)
            nc.vector.scalar_tensor_tensor(peak[:, 0:2], bqk_peak[:, :], BIAS_SHARE, w_peak[:, :], ALU.mult, ALU.max).then_inc(peak_done, 1)
            dve.wait_ge(peak_all_done, 1)
            nc.vector.tensor_scalar(peak_min[:, :], peak_all[:, :], 2.0 ** -40, None, ALU.max).then_inc(scale_step, 1)
            dve.wait_ge(scale_step, 1)
            nc.vector.tensor_scalar(pow2[:, :].bitcast(U32), peak_min[:, :].bitcast(U32), EXP_BITS, None,
                                    ALU.bitwise_and).then_inc(scale_step, 1)
            dve.wait_ge(scale_step, 2)
            nc.vector.reciprocal(pow2_inv[:, :], pow2[:, :]).then_inc(scale_step, 1)
            dve.wait_ge(scale_step, 3)
            nc.vector.tensor_scalar(pow2_inv15[:, :], pow2_inv[:, :], 1.5, None, ALU.mult).then_inc(scale_step, 1)
            dve.wait_ge(scale_step, 4)
            nc.vector.tensor_scalar(pow2_invx[:, :].bitcast(U32), pow2_inv15[:, :].bitcast(U32), EXP_BITS, None,
                                    ALU.bitwise_and).then_inc(scale_step, 1)
            dve.wait_ge(scale_step, 5)
            nc.vector.tensor_scalar(up[:, :], pow2_invx[:, :], W_SCALE, None, ALU.mult).then_inc(scale_done, 1)
            nc.vector.tensor_scalar(down[:, :], pow2[:, :], 1.0 / (W_SCALE * H_SCALE), None, ALU.mult).then_inc(scale_done, 1)
            dve.wait_ge(scale_done, 2)
            nc.vector.tensor_scalar(undo[:, :], down[:, 0:3], 1.0 / P_SCALE, None, ALU.mult).then_inc(scale_done, 1)
            nc.vector.tensor_scalar(redo[:, :], up[:, 0:2], H_SCALE * P_SCALE, None, ALU.mult).then_inc(scale_done, 1)
            dve.wait_ge(scale_done, 4)
            nc.vector.tensor_tensor(score_scale[:, :], undo[:, 0:1], undo[:, 1:2], ALU.mult).then_inc(scale_done, 1)
            nc.vector.tensor_tensor(bqk_up[:, :, :], bqk[:, :, :], redo[:, :].unsqueeze(2).to_broadcast([P, 2, KC]),
                                    ALU.mult).then_inc(scale_done, 1)
            dve.wait_ge(heads_done, 1)
            nc.vector.scalar_tensor_tensor(adjT[:, 1, :], ring[:, 0, 0:P], up[:, 3:4], adjT[:, 0, :],
                                           ALU.mult, ALU.subtract).then_inc(rests_done, 1)
            for k in range(1, GROUP):
                stats_of(0, k)
                moments_wait(0, k)
                moments_of(0, k)
            for j in range(3):
                dve.wait_ge(heads_done, j + 2)
                nc.vector.scalar_tensor_tensor(w16[:, j, 1, :, :].rearrange("p c n -> p (c n)"),
                                               w_raw[:, j, :, :].rearrange("p c n -> p (c n)"), up[:, j:j + 1],
                                               w16[:, j, 0, :, :].rearrange("p c n -> p (c n)"),
                                               ALU.mult, ALU.subtract).then_inc(rests_done, 1)
            for k in range(GROUP, MOMENTS_AHEAD):
                stats_of(0, k)
                moments_wait(0, k)
                moments_of(0, k)
            for k in range(PREP_AHEAD):
                transpose_out(0, k, 2 * k % 4)
                adjacency_out(0, k, (2 * k + 1) % 4)
            dve.wait_ge(mask_done, 2)
            dve.wait_ge(scale_done, 6)

            def slot(base, k):
                transpose_out(base, k + PREP_AHEAD, ring_place(k, 0))
                softmax_shift(base, k - ATTN_BEHIND)
                v_rest(base, k - 1)
                attention_out(base, k - OUT_BEHIND)
                stats_of(base, k + MOMENTS_AHEAD)
                moments_wait(base, k + MOMENTS_AHEAD)
                adjacency_out(base, k + PREP_AHEAD, ring_place(k, 3))
                moments_of(base, k + MOMENTS_AHEAD)
                probs_rest(base, k - ATTN_BEHIND)

            slots(dve, slot)
            v_rest(B, -1)
            attention_out(B, -OUT_BEHIND)
            softmax_shift(*TAIL[0], pairs_of_banks[0])
            for i, graph in enumerate(TAIL):
                if i + 1 < len(TAIL):
                    softmax_shift(*TAIL[i + 1], pairs_of_banks[(i + 1) % 2])
                probs_rest(*graph, pairs_of_banks[i % 2])
                attention_out(*graph)

        @block.tensor
        def _(pe):
            PAIRS = ((0, 0), (0, 1), (1, 0))

            def transposes(base, k, place):
                if in_range(base, k):
                    pe.wait_ge(h_rest_done, base + k + 1)
                    t = ring[:, place, :].bitcast(F16)
                    for s in range(2):
                        for c in range(KC):
                            i = s * KC + c
                            last = nc.tensor.transpose(t[:, i * P:(i + 1) * P], h16[:, k % 4, s, c * P:(c + 1) * P], ident16[:, :])
                    last.then_inc(t_ready, 1)

            def adjacency(base, k, place):
                if in_range(base, k):
                    for i, (s, t) in enumerate(PAIRS):
                        last = nc.tensor.matmul(ring[:, place, :], adjT[:, s, :], h16[:, k % 4, t, :],
                                                start=(i == 0), stop=(i == 2))
                    last.then_inc(a_ready, 1)

            def qk_chunk(base, k, u, place):
                if in_range(base, k):
                    j, col = u // KC, u % KC
                    for c in range(KC):
                        for i, (s, t) in enumerate(PAIRS):
                            last = nc.tensor.matmul(ring[:, place, :], w16[:, j, s, c, col * P:(col + 1) * P],
                                                    hT[:, k // GROUP % 2, t, c, :, :].rearrange("p g n -> p (g n)"),
                                                    start=(c == 0 and i == 0), stop=(c == KC - 1 and i == 2))
                    last.then_inc(qk_ready, 1)

            def v_rows(base, k, place):
                if in_range(base, k):
                    for c in range(KC):
                        for i, (s, t) in enumerate(PAIRS):
                            last = nc.tensor.matmul(ring[:, place, :], hT[:, k // GROUP % 2, s, c, k % GROUP, :],
                                                    w16[:, 2, t, c, :], start=(c == 0 and i == 0),
                                                    stop=(c == KC - 1 and i == 2))
                    last.then_inc(v_ready, 1)

            def scores(base, k, banks=sc, in_tail=False):
                if in_range(base, k):
                    m = base + k
                    pe.wait_ge(qk_rest_done, 2 * (m - k % GROUP + GROUP))
                    if not in_tail:
                        wait(pe, pt_evac, m)
                    for c in range(KC):
                        for i, (s, t) in enumerate(PAIRS):
                            for half in range(2):
                                rows = slice(half * HD, half * HD + HD)
                                last = nc.tensor.matmul(banks[:, half, c * P:(c + 1) * P],
                                                        qkT[rows, k // GROUP % 2, s, 0, c, k % GROUP, :],
                                                        qkT[rows, k // GROUP % 2, t, 1, c, k % GROUP, :],
                                                        start=(i == 0), stop=(i == 2))
                    last.then_inc(s_ready, 1)

            def probs_transposed(base, k, banks=sc):
                if in_range(base, k):
                    pe.wait_ge(probs_done, base + k + 1)
                    for i in range(H):
                        last = nc.tensor.transpose(banks[:, i // 4, i % 4 * P:(i % 4 + 1) * P], probs[:, i, :], ident[:, :])
                    last.then_inc(pt_ready, 1)

            def probs_times_v(base, k):
                if in_range(base, k):
                    m = base + k
                    pe.wait_ge(pt_evac, m + 1)
                    pe.wait_ge(v_evac, m + 1)
                    wait(pe, o_evac, m)
                    for h in range(H):
                        for i, (s, t) in enumerate(PAIRS):
                            w = HD if t else VW
                            last = nc.tensor.matmul(o_view[:, h // 4, h % 4, 0:w], probsT[:, s, h % 2 * 4 + h // 2, :],
                                                    v16[:, t, k // GROUP % 2, k % GROUP, h, 0:w],
                                                    start=(i == 0), stop=(i == 2))
                    last.then_inc(o_ready, 1)

            pe.wait_ge(ident_step, 2)
            pe.wait_ge(adj_loaded, 16)
            nc.tensor.transpose(ring[:, 0, 0:P], adj_sb[:, :], ident[:, :]).then_inc(adjT_ready, 1)
            pe.wait_ge(rests_done, 1)
            pe.wait_ge(pool_const, 5)
            for k in range(PREP_AHEAD):
                if k >= 2:
                    pe.wait_ge(t_evac, k - 1)
                    pe.wait_ge(a_evac, k - 1)
                transposes(0, k, 2 * k % 4)
                adjacency(0, k, (2 * k + 1) % 4)
            pe.wait_ge(rests_done, 4)

            def slot(base, k):
                n = base + k
                u = 2 * (k % GROUP)
                if isinstance(base, int) and n == 0:
                    pe.wait_ge(t_evac, PREP_AHEAD)
                    pe.wait_ge(a_evac, PREP_AHEAD)
                if in_range(base, k + PREP_AHEAD):
                    wait(pe, qk_evac, 2 * n - 1)
                transposes(base, k + PREP_AHEAD, ring_place(k, 0))
                scores(base, k - ATTN_BEHIND)
                if in_range(base, k):
                    if k % GROUP == 0:
                        pe.wait_ge(t_evac, n + GROUP)
                    wait(pe, qk_evac, 2 * n)
                qk_chunk(base, k, u, ring_place(k, 1))
                if in_range(base, k):
                    pe.wait_ge(a_evac, n + PREP_AHEAD if not isinstance(base, int) else min(n + PREP_AHEAD, B))
                qk_chunk(base, k, u + 1, ring_place(k, 2))
                probs_transposed(base, k - ATTN_BEHIND)
                if in_range(base, k + PREP_AHEAD):
                    wait(pe, v_evac, n)
                adjacency(base, k + PREP_AHEAD, ring_place(k, 3))
                if in_range(base, k):
                    wait(pe, t_evac, n + PREP_AHEAD + 1 if not isinstance(base, int) else min(n + PREP_AHEAD + 1, B))
                    wait(pe, qk_evac, 2 * n - 1)
                v_rows(base, k, ring_place(k, 4))
                probs_times_v(base, k - ATTN_BEHIND)

            slots(pe, slot)
            scores(*TAIL[0])
            pe.wait_ge(v_evac, B)
            pe.wait_ge(qk_evac, 2 * B)
            pe.wait_ge(t_evac, B)
            pe.wait_ge(a_evac, B)
            for i, (base, k) in enumerate(TAIL):
                if i + 1 < len(TAIL):
                    if i:
                        pe.wait_ge(pt_evac, base + k)
                    scores(*TAIL[i + 1], pairs_of_banks[(i + 1) % 2], in_tail=True)
                probs_transposed(base, k, pairs_of_banks[i % 2])
                probs_times_v(base, k)


_INS = ["x", "adj", "L0_gnn_b", "L1_gnn_Wq", "L1_gnn_bq", "L1_gnn_Wk", "L1_gnn_bk", "L1_gnn_Wv", "L1_gnn_bv"]


def kernel(**inputs):
    import concourse.bacc as _bacc
    from concourse.bass_utils import run_bass_kernel_spmd as _run

    nc = _bacc.Bacc("TRN2", target_bir_lowering=False, num_devices=1)
    arrays, args = {}, []
    for name in _INS:
        a = np.ascontiguousarray(inputs[name])
        arrays[f"in_{name}"] = a
        args.append(nc.dram_tensor(f"in_{name}", a.shape, mybir.dt.from_np(a.dtype), kind="ExternalInput").ap())
    out = nc.dram_tensor("out_x", inputs["x"].shape, F32, kind="ExternalOutput").ap()
    graph_layers(nc, *args, out)
    r = _run(nc, [arrays], core_ids=[0])
    return r.results[0]["out_x"]
```

```python
from contextlib import ExitStack

import numpy as np
import concourse.bass as bass
from concourse import mybir

ALU = mybir.AluOpType
ACT = mybir.ActivationFunctionType
F32 = mybir.dt.float32
F16 = mybir.dt.float16
U32 = mybir.dt.uint32
AX = mybir.AxisListType

P = 128
H, HD = 8, 64
GROUP = 4
RING = 8
H_SCALE = 2.0 ** 11
W_SCALE = 2.0 ** 14
P_SCALE = 2.0 ** -21
BIAS_SHARE = 2.0 ** -8
EXP_BITS = 0x7F800000
LOAD_AHEAD, MOMENTS_AHEAD, NORM_AHEAD, TURN_AHEAD, PREP_AHEAD, X1_AHEAD = 8, 6, 5, 5, 4, 1
ATTN_BEHIND, OUT_BEHIND, STORE_BEHIND = 5, 6, 7


def graph_layers(nc, x, adj, b0, wq, bq, wk, bk, wv, bv, out):
    B, N, D = x.shape
    assert N == P and D == H * HD and B % (2 * GROUP) == 0
    KC = D // P
    VW = HD + 1
    VP = HD + 2

    with ExitStack() as ctx:
        def sb(name, shape, dt=F32):
            return ctx.enter_context(nc.sbuf_tensor(name, shape, dt))

        def ps(name, shape, dt=F32):
            return ctx.enter_context(nc.psum_tensor(name, shape, dt))

        def sem(name):
            return ctx.enter_context(nc.semaphore(name))

        ident = sb("ident", [P, P])
        ones = sb("ones", [P, P])
        adj_sb = sb("adj_sb", [P, P])
        mask8 = sb("mask8", [P, P])
        adjT = sb("adjT", [P, 2, P], F16)
        w_raw = sb("w_raw", [P, 3, KC, D])
        w16 = sb("w16", [P, 3, 2, KC, D], F16)
        bqk = sb("bqk", [P, 2, KC])
        b0_col = sb("b0_col", [P, 1])
        bv_rows = sb("bv_rows", [P, D])
        peak = sb("peak", [P, 4])
        peak_all = sb("peak_all", [P, 4])
        peak_min = sb("peak_min", [P, 4])
        pow2 = sb("pow2", [P, 4])
        pow2_inv = sb("pow2_inv", [P, 4])
        pow2_inv15 = sb("pow2_inv15", [P, 4])
        pow2_invx = sb("pow2_invx", [P, 4])
        up = sb("up", [P, 4])
        down = sb("down", [P, 4])
        undo = sb("undo", [P, 3])
        redo = sb("redo", [P, 2])
        score_scale = sb("score_scale", [P, 1])
        bqk_peak = sb("bqk_peak", [P, 2])
        w_peak = sb("w_peak", [P, 2])
        bqk_up = sb("bqk_up", [P, 2, KC])
        minus_half = sb("minus_half", [P, 1])
        eps = sb("eps", [P, 1])
        plus_minus = sb("plus_minus", [P, 2])
        x_in = sb("x_in", [P, RING, D])
        xbv = sb("xbv", [P, D])
        x1 = sb("x1", [P, RING, D])
        y = sb("y", [P, 2, D])
        stats = sb("stats", [P, 2, 6])
        mean_var = sb("mean_var", [P, 2, 2])
        var_eps = sb("var_eps", [P, 2, 1])
        inv_std = sb("inv_std", [P, 2, 1])
        h_mul = sb("h_mul", [P, 2, 2])
        h_add = sb("h_add", [P, 2, 1])
        h32 = sb("h32", [P, 2, D])
        h16 = sb("h16", [P, 4, 2, D], F16)
        hT = sb("hT", [P, 2, 2, KC, GROUP, P], F16)
        a_max = sb("a_max", [P, RING, 1])
        c_col = sb("c_col", [P, RING, 1])
        qk32 = sb("qk32", [P, 2, GROUP * P])
        qkT = sb("qkT", [P, 2, 2, 2, KC, GROUP, P], F16)
        v16 = sb("v16", [P, 2, 2, GROUP, H, VP], F16)
        masked = sb("masked", [P, H, P])
        row_max = sb("row_max", [P, H])
        shifted = sb("shifted", [P, H, P])
        probs = sb("probs", [P, H, P])
        probs16 = sb("probs16", [P, 2, H, P], F16)
        probsT = sb("probsT", [P, 2, H, P], F16)
        inv_sum = sb("inv_sum", [P, 2, H // 2])
        out_scale = sb("out_scale", [P, 2, H // 2])
        attn = sb("attn", [P, 2, D])
        proj = ps("proj", [P, 4, 512])
        A_BANK, V_BANK = 2, 3
        sc = ps("sc", [P, 2, 512])
        o_ps = ps("o_ps", [P, 2, 512])
        o_view = o_ps[:, :, 0:H // 2 * VW].rearrange("p t (h e) -> p t h e", e=VW)

        x_loaded = [sem(f"x_loaded{i}") for i in range(RING)]
        y_stored = [sem(f"y_stored{i}") for i in range(2)]
        adj_loaded, bias_loaded = sem("adj_loaded"), sem("bias_loaded")
        w_loaded = [sem(f"w_loaded{j}") for j in range(3)]
        ident_step, pool_const = sem("ident_step"), sem("pool_const")
        peak_done, peak_all_done, scale_step, scale_done = sem("peak_done"), sem("peak_all_done"), sem("scale_step"), sem("scale_done")
        w_peak_done, down_done, undo_done, redo_done, bias_done, score_scale_done = (
            sem("w_peak_done"), sem("down_done"), sem("undo_done"), sem("redo_done"), sem("bias_done"), sem("score_scale_done"))
        mask_done, adjT_ready, heads_done, rests_done = sem("mask_done"), sem("adjT_ready"), sem("heads_done"), sem("rests_done")
        bn_done, mv_done, norm_step, norm_done = sem("bn_done"), sem("mv_done"), sem("norm_step"), sem("norm_done")
        h32_done, h_head_done, h_rest_done = sem("h32_done"), sem("h_head_done"), sem("h_rest_done")
        hT_done = [sem(f"hT_done{i}") for i in range(GROUP)]
        a_ready, a_evac = sem("a_ready"), sem("a_evac")
        qk_ready, qk_evac, qk_head_done, qk_rest_done = sem("qk_ready"), sem("qk_evac"), sem("qk_head_done"), sem("qk_rest_done")
        v_ready, v_head_done, v_evac = sem("v_ready"), sem("v_head_done"), sem("v_evac")
        s_ready, masked_done, max_done, shifted_done, probs_done = (
            sem("s_ready"), sem("masked_done"), sem("max_done"), sem("shifted_done"), sem("probs_done"))
        probs_head_done, probs_rest_done, probsT_done = sem("probs_head_done"), sem("probs_rest_done"), sem("probsT_done")
        o_ready, inv_sum_done, out_scale_done, o_evac = sem("o_ready"), sem("inv_sum_done"), sem("out_scale_done"), sem("o_evac")
        c_done, xc_done, x1_done, y_done = sem("c_done"), sem("xc_done"), sem("x1_done"), sem("y_done")

        def wait(eng, s, count):
            if not isinstance(count, int) or count > 0:
                eng.wait_ge(s, count)

        def in_range(base, k):
            return not isinstance(base, int) or 0 <= base + k < B

        def qk_place(k, u, part):
            return qkT[:, k // GROUP % 2, part, u // KC, u % KC, :, :].rearrange("p g n -> p (g n)")

        MATRICES = (3, 0, 2, 1)
        TAIL = [(B, k) for k in range(-ATTN_BEHIND, 0)]
        pairs_of_banks = (sc, proj[:, 0:2, :])

        def wait_transposed(eng, base, k):
            eng.wait_ge(hT_done[k % GROUP], 4 * (base + k - k % GROUP) + 16)

        def slots(eng, slot, after_first=None):
            for k in range(RING):
                slot(0, k)
                if k == 0 and after_first:
                    after_first()
            with eng.Fori(RING, B - 2 * RING + 1, RING) as base:
                for k in range(RING):
                    slot(base, k)
            for k in range(RING):
                slot(B - RING, k)

        block = ctx.enter_context(nc.Block())

        @block.sync
        def _(sp):
            def load(base, k):
                if in_range(base, k):
                    wait(sp, x1_done, base + k - RING + 1)
                    sp.dma_start(x_in[:, k % RING, :], x[base + k, :, :]).then_inc(x_loaded[k % RING], 16)

            def store(base, k):
                if in_range(base, k):
                    sp.wait_ge(y_done, base + k + 1)
                    sp.dma_start(out[base + k, :, :], y[:, k % 2, :]).then_inc(y_stored[k % 2], 16)

            load(0, 0)
            sp.dma_start(adj_sb[:, :], adj).then_inc(adj_loaded, 16)
            for k in range(1, PREP_AHEAD):
                load(0, k)
            for j, w in ((0, wq), (2, wv), (1, wk)):
                sp.dma_start(w_raw[:, j, :, :], w.rearrange("(c p) n -> p c n", p=P)).then_inc(w_loaded[j], 16)
            for k in range(PREP_AHEAD, LOAD_AHEAD):
                load(0, k)

            def transpose(base, k):
                if in_range(base, k):
                    sp.dma_start_transpose(
                        hT[:, k // GROUP % 2, :, :, k % GROUP, :].rearrange("p s c n -> p (s c) n"),
                        h16[:, k % 4, :, :].rearrange("p s n -> p (s n)")).then_inc(hT_done[k % GROUP], 16)

            def transpose_probs(base, k):
                if in_range(base, k):
                    sp.dma_start_transpose(probsT[:, :, :, :].rearrange("p s h n -> p (s h) n"),
                                           probs16[:, :, :, :].rearrange("p s h n -> p (s h n)")).then_inc(probsT_done, 16)

            def slot(base, k):
                if isinstance(base, int):
                    load(base, k + LOAD_AHEAD)
                else:
                    sp.wait_ge(o_evac, base + k - OUT_BEHIND + 1)
                    sp.dma_start(x_in[:, k % RING, :], x[base + k + LOAD_AHEAD, :, :]).then_inc(x_loaded[k % RING], 16)
                if isinstance(base, int) and in_range(base, k - ATTN_BEHIND):
                    sp.wait_ge(probs_rest_done, base + k - ATTN_BEHIND + 1)
                    wait(sp, o_ready, base + k - ATTN_BEHIND)
                transpose_probs(base, k - ATTN_BEHIND)
                if isinstance(base, int) and in_range(base, k + TURN_AHEAD):
                    m = base + k + TURN_AHEAD
                    sp.wait_ge(h_rest_done, m + 1)
                    wait(sp, qk_ready, 2 * (m - m % GROUP - GROUP))
                    wait(sp, v_ready, m + 1 - 2 * GROUP)
                transpose(base, k + TURN_AHEAD)
                store(base, k - STORE_BEHIND)

            for k in range(TURN_AHEAD):
                sp.wait_ge(h_rest_done, k + 1)
                transpose(0, k)

            slots(sp, slot)
            for k in range(-ATTN_BEHIND, 0):
                sp.wait_ge(probs_rest_done, B + k + 1)
                sp.wait_ge(o_ready, B + k)
                transpose_probs(B, k)
                store(B, k - 2)
            store(B, -2)
            store(B, -1)
            for k in range(2):
                sp.wait_ge(y_stored[k], 16 * (B // 2))

        @block.gpsimd
        def _(pool):
            pool.memset(ident[:, :], 0.0).then_inc(ident_step, 1)
            pool.memset(minus_half[:, :], -0.5).then_inc(pool_const, 1)
            pool.memset(eps[:, :], 1e-5).then_inc(pool_const, 1)
            pool.memset(plus_minus[:, 0:1], H_SCALE).then_inc(pool_const, 1)
            pool.memset(plus_minus[:, 1:2], -H_SCALE).then_inc(pool_const, 1)
            pool.wait_ge(ident_step, 1)
            pool.affine_select(out=ident[:, :], in_=ident[:, :], compare_op=ALU.not_equal, fill=1.0, base=0,
                               pattern=[[-1, P]], channel_multiplier=1).then_inc(ident_step, 1)
            pool.wait_ge(pool_const, 4)

            def norm_scales(base, k):
                if in_range(base, k):
                    r = k % 2
                    m = base + k
                    pool.wait_ge(mv_done, m + 1)
                    pool.tensor_tensor(var_eps[:, r, :], mean_var[:, r, 1:2], eps[:, :], ALU.add).then_inc(norm_step, 1)
                    pool.wait_ge(norm_step, 3 * m + 1)
                    pool.tensor_tensor(inv_std[:, r, :], var_eps[:, r, :], minus_half[:, :],
                                       ALU.pow).then_inc(norm_step, 1)
                    pool.wait_ge(norm_step, 3 * m + 2)
                    wait(pool, h_head_done, m - 1)
                    wait(pool, h32_done, m - 1)
                    pool.tensor_tensor(h_mul[:, r, :], inv_std[:, r, :].to_broadcast([P, 2]), plus_minus[:, :],
                                       ALU.mult).then_inc(norm_step, 1)
                    pool.wait_ge(norm_step, 3 * m + 3)
                    pool.tensor_tensor(h_add[:, r, :], mean_var[:, r, 0:1], h_mul[:, r, 1:2],
                                       ALU.mult).then_inc(norm_done, 1)

            def rest(base, k):
                if in_range(base, k):
                    pool.wait_ge(h32_done, base + k + 1)
                    pool.wait_ge(h_head_done, base + k + 1)
                    if in_range(base, k - 4):
                        pool.wait_ge(a_ready, base + k - 3)
                        wait_transposed(pool, base, k - 4)
                    pool.tensor_tensor(h16[:, k % 4, 1, :], h32[:, k % 2, :], h16[:, k % 4, 0, :],
                                       ALU.subtract).then_inc(h_rest_done, 1)

            def finish(base, k):
                if in_range(base, k):
                    m = base + k
                    pool.wait_ge(o_evac, m + 1)
                    pool.wait_ge(x1_done, m + 1)
                    wait(pool, y_stored[k % 2], (m - k % 2) * 8)
                    pool.tensor_tensor(y[:, k % 2, :], attn[:, k % 2, :], x1[:, k % RING, :],
                                       ALU.add).then_inc(y_done, 1)

            def add_c(base, k):
                if in_range(base, k):
                    m = base + k
                    wait(pool, y_done, m - RING + 1)
                    wait(pool, x1_done, m)
                    pool.tensor_tensor(xbv[:, :], x_in[:, k % RING, :], bv_rows[:, :], ALU.add).then_inc(xc_done, 1)
                    pool.wait_ge(xc_done, m + 1)
                    pool.wait_ge(c_done, m + 1)
                    pool.tensor_tensor(x1[:, k % RING, :], xbv[:, :],
                                       c_col[:, k % RING, :].to_broadcast([P, D]), ALU.add).then_inc(x1_done, 1)

            def qk_rest(base, k, u):
                if in_range(base, k):
                    count = 2 * (base + k) + u % 2 + 1
                    pool.wait_ge(qk_evac, count)
                    pool.wait_ge(qk_head_done, count)
                    pool.tensor_tensor(qk_place(k, u, 1), qk32[:, u % 2, :], qk_place(k, u, 0),
                                       ALU.subtract).then_inc(qk_rest_done, 1)

            def peak_over_rows(i):
                c = MATRICES[i]
                pool.wait_ge(peak_done, i + 1)
                pool.partition_all_reduce(peak_all[:, c:c + 1], peak[:, c:c + 1], P,
                                          bass.bass_isa.ReduceOp.max).then_inc(peak_all_done, 1)

            norm_scales(0, 0)
            peak_over_rows(0)
            norm_scales(0, 1)
            rest(0, 0)
            norm_scales(0, 2)
            rest(0, 1)
            norm_scales(0, 3)
            rest(0, 2)
            peak_over_rows(1)
            rest(0, 3)
            peak_over_rows(2)
            norm_scales(0, 4)
            rest(0, 4)
            norm_scales(0, 5)
            peak_over_rows(3)
            pool.wait_ge(bias_loaded, 64)
            for k in range(X1_AHEAD):
                add_c(0, k)
            assert (NORM_AHEAD, MOMENTS_AHEAD) == (5, 6)

            def slot(base, k):
                u = 2 * (k % GROUP)
                add_c(base, k + X1_AHEAD)
                rest(base, k + NORM_AHEAD)
                qk_rest(base, k, u)
                norm_scales(base, k + MOMENTS_AHEAD)
                qk_rest(base, k, u + 1)
                finish(base, k - OUT_BEHIND)

            slots(pool, slot)
            for k in range(-OUT_BEHIND, 0):
                finish(B, k)

        @block.scalar
        def _(act):
            def normalise(base, k):
                if in_range(base, k):
                    m = base + k
                    act.wait_ge(norm_done, m + 1)
                    wait(act, h_rest_done, m - 1)
                    if in_range(base, k - 4):
                        act.wait_ge(a_ready, m - 3)
                        wait_transposed(act, base, k - 4)
                    args = dict(scale=h_mul[:, k % 2, 0:1], bias=h_add[:, k % 2, :])
                    nc.scalar.activation(h32[:, k % 2, :], x_in[:, k % RING, :], ACT.Relu, **args).then_inc(h32_done, 1)
                    nc.scalar.activation(h16[:, k % 4, 0, :], x_in[:, k % RING, :], ACT.Relu, **args).then_inc(h_head_done, 1)

            def qk_out(base, k, u):
                if in_range(base, k):
                    count = 2 * (base + k) + u % 2 + 1
                    if isinstance(base, int) and base == 0 and k % GROUP % 2 == 0 and k < GROUP:
                        act.wait_ge(bias_done, u // KC + 1)
                    act.wait_ge(qk_ready, count)
                    place = proj[:, u % 2, :]
                    bias = bqk_up[:, u // KC, u % KC:u % KC + 1]
                    nc.scalar.activation(qk_place(k, u, 0), place, ACT.Identity, scale=P_SCALE, bias=bias).then_inc(qk_head_done, 1)
                    wait(act, qk_rest_done, count - 2)
                    nc.scalar.activation(qk32[:, u % 2, :], place, ACT.Identity, scale=P_SCALE, bias=bias).then_inc(qk_evac, 1)

            def v_head(base, k):
                if in_range(base, k):
                    act.wait_ge(v_ready, base + k + 1)
                    nc.scalar.activation(v16[:, 0, k // GROUP % 2, k % GROUP, :, 0:HD],
                                         proj[:, V_BANK, :].rearrange("p (h d) -> p h d", d=HD),
                                         ACT.Copy, scale=P_SCALE).then_inc(v_head_done, 1)

            def exps(base, k):
                if in_range(base, k):
                    m = base + k
                    act.wait_ge(shifted_done, m + 1)
                    wait(act, probsT_done, m * 16)
                    nc.scalar.activation(probs16[:, 0, :, :], shifted[:, :, :], ACT.Exp, scale=HD ** -0.5).then_inc(probs_head_done, 1)
                    wait(act, probs_rest_done, m)
                    nc.scalar.activation(probs[:, :, :], shifted[:, :, :], ACT.Exp, scale=HD ** -0.5).then_inc(probs_done, 1)

            def c_of(base, k):
                if in_range(base, k):
                    m = base + k
                    if isinstance(base, int) and m == 0:
                        act.wait_ge(down_done, 1)
                    act.wait_ge(a_evac, m + 1)
                    wait(act, x1_done, m - RING + 1)
                    nc.scalar.activation(c_col[:, k % RING, :], a_max[:, k % RING, :], ACT.Relu, scale=down[:, 3:4],
                                         bias=b0_col[:, :]).then_inc(c_done, 1)

            def w_head(j, batch):
                act.wait_ge(scale_done, batch + 1)
                nc.scalar.activation(w16[:, j, 0, :, :], w_raw[:, j, :, :], ACT.Identity, scale=up[:, j:j + 1]).then_inc(heads_done, 1)

            act.dma_start(b0_col[:, :], b0.rearrange("(p a) -> p a", a=1)).then_inc(bias_loaded, 16)
            act.dma_start(bqk[:, 0, :], bq.rearrange("(c p) -> p c", p=P), allow_slow_non_contiguous=True).then_inc(bias_loaded, 16)
            act.dma_start(bqk[:, 1, :], bk.rearrange("(c p) -> p c", p=P), allow_slow_non_contiguous=True).then_inc(bias_loaded, 16)
            act.dma_start(bv_rows[:, :], bv.partition_broadcast(P)).then_inc(bias_loaded, 16)
            normalise(0, 0)
            act.wait_ge(scale_done, 1)
            act.wait_ge(adjT_ready, 1)
            nc.scalar.activation(adjT[:, 0, :], proj[:, A_BANK, 0:P], ACT.Identity, scale=up[:, 3:4]).then_inc(heads_done, 1)
            for k in range(1, PREP_AHEAD):
                normalise(0, k)
            w_head(0, 1)
            normalise(0, 4)
            w_head(2, 2)
            act.wait_ge(bias_loaded, 64)
            for k in range(X1_AHEAD):
                c_of(0, k)

            def slot(base, k):
                u = 2 * (k % GROUP)
                v_head(base, k - 1)
                c_of(base, k + X1_AHEAD)
                normalise(base, k + NORM_AHEAD)
                qk_out(base, k, u)
                exps(base, k - ATTN_BEHIND)
                qk_out(base, k, u + 1)

            slots(act, slot, after_first=lambda: w_head(1, 3))
            v_head(B, -1)
            for graph in TAIL:
                exps(*graph)

        @block.vector
        def _(dve):
            def stats_of(base, k):
                if in_range(base, k):
                    m = base + k
                    dve.wait_ge(x_loaded[k % RING], 16 * 1 + (m - k % RING) * 2)
                    nc.vector.bn_stats(stats[:, k % 2, :], x_in[:, k % RING, :]).then_inc(bn_done, 1)

            def moments_wait(base, k):
                if in_range(base, k):
                    dve.wait_ge(bn_done, base + k + 1)
                    wait(dve, norm_done, base + k - 1)

            def moments_of(base, k):
                if in_range(base, k):
                    nc.vector.bn_aggr(mean_var[:, k % 2, :], stats[:, k % 2, :]).then_inc(mv_done, 1)

            def adjacency_out(base, k):
                if in_range(base, k):
                    m = base + k
                    dve.wait_ge(a_ready, m + 1)
                    wait(dve, c_done, m - RING + 1)
                    nc.vector.tensor_reduce(a_max[:, k % RING, :], proj[:, A_BANK, :], AX.X, ALU.max).then_inc(a_evac, 1)

            def v_rest(base, k):
                if in_range(base, k):
                    dve.wait_ge(v_head_done, base + k + 1)
                    nc.vector.scalar_tensor_tensor(
                        v16[:, 1, k // GROUP % 2, k % GROUP, :, 0:HD],
                        proj[:, V_BANK, :].rearrange("p (h d) -> p h d", d=HD), P_SCALE,
                        v16[:, 0, k // GROUP % 2, k % GROUP, :, 0:HD], ALU.mult, ALU.subtract).then_inc(v_evac, 1)

            def probs_rest(base, k):
                if in_range(base, k):
                    dve.wait_ge(probs_head_done, base + k + 1)
                    dve.wait_ge(probs_done, base + k + 1)
                    nc.vector.tensor_tensor(probs16[:, 1, :, :], probs[:, :, :], probs16[:, 0, :, :],
                                            ALU.subtract).then_inc(probs_rest_done, 1)

            def softmax_shift(base, k, banks=sc):
                if in_range(base, k):
                    m = base + k
                    wait(dve, shifted_done, m)
                    dve.wait_ge(s_ready, m + 1)
                    nc.vector.scalar_tensor_tensor(masked[:, :, :], banks[:, :, :].rearrange("p t (h n) -> p (t h) n", n=P),
                                                   score_scale[:, :], mask8[:, :].unsqueeze(1).to_broadcast([P, H, P]),
                                                   ALU.mult, ALU.add).then_inc(masked_done, 1)
                    dve.wait_ge(masked_done, m + 1)
                    nc.vector.tensor_reduce(row_max[:, :], masked[:, :, :], AX.X, ALU.max).then_inc(max_done, 1)
                    dve.wait_ge(max_done, m + 1)
                    wait(dve, probs_done, m)
                    nc.vector.tensor_tensor(shifted[:, :, :], masked[:, :, :],
                                            row_max[:, :].unsqueeze(2).to_broadcast([P, H, P]), ALU.subtract).then_inc(shifted_done, 1)

            def attention_out(base, k):
                if in_range(base, k):
                    m = base + k
                    if in_range(base, k + OUT_BEHIND + NORM_AHEAD):
                        dve.wait_ge(h_rest_done, m + OUT_BEHIND + NORM_AHEAD + 1)
                    dve.wait_ge(o_ready, m + 1)
                    nc.vector.reciprocal(inv_sum[:, :, :], o_view[:, :, :, HD]).then_inc(inv_sum_done, 1)
                    dve.wait_ge(inv_sum_done, m + 1)
                    nc.vector.tensor_scalar(out_scale[:, :, :], inv_sum[:, :, :], undo[:, 2:3], None,
                                            ALU.mult).then_inc(out_scale_done, 1)
                    dve.wait_ge(out_scale_done, m + 1)
                    wait(dve, y_done, m - 1)
                    nc.vector.tensor_tensor(attn[:, k % 2, :].rearrange("p (t h d) -> p t h d", t=2, d=HD),
                                            o_view[:, :, :, 0:HD],
                                            out_scale[:, :, :].unsqueeze(3).to_broadcast([P, 2, H // 2, HD]),
                                            ALU.mult).then_inc(o_evac, 1)

            def moments(k):
                stats_of(0, k)
                moments_wait(0, k)
                moments_of(0, k)

            def w_peak_of(j, i):
                dve.wait_ge(w_loaded[j], 16)
                flat = w_raw[:, j, :, :].rearrange("p c n -> p (c n)")
                if j == 2:
                    nc.vector.tensor_reduce(peak[:, 2:3], flat, AX.X, ALU.max, apply_absolute_value=True).then_inc(peak_done, 1)
                    return
                nc.vector.tensor_reduce(w_peak[:, j:j + 1], flat, AX.X, ALU.max, apply_absolute_value=True).then_inc(w_peak_done, 1)
                dve.wait_ge(w_peak_done, 2 + j)
                nc.vector.scalar_tensor_tensor(peak[:, j:j + 1], bqk_peak[:, j:j + 1], BIAS_SHARE, w_peak[:, j:j + 1],
                                               ALU.mult, ALU.max).then_inc(peak_done, 1)

            def scales_of(i):
                c = slice(MATRICES[i], MATRICES[i] + 1)
                dve.wait_ge(peak_all_done, i + 1)
                nc.vector.tensor_scalar(peak_min[:, c], peak_all[:, c], 2.0 ** -40, None, ALU.max).then_inc(scale_step, 1)
                dve.wait_ge(scale_step, 5 * i + 1)
                nc.vector.tensor_scalar(pow2[:, c].bitcast(U32), peak_min[:, c].bitcast(U32), EXP_BITS, None,
                                        ALU.bitwise_and).then_inc(scale_step, 1)
                dve.wait_ge(scale_step, 5 * i + 2)
                nc.vector.reciprocal(pow2_inv[:, c], pow2[:, c]).then_inc(scale_step, 1)
                dve.wait_ge(scale_step, 5 * i + 3)
                nc.vector.tensor_scalar(pow2_inv15[:, c], pow2_inv[:, c], 1.5, None, ALU.mult).then_inc(scale_step, 1)
                dve.wait_ge(scale_step, 5 * i + 4)
                nc.vector.tensor_scalar(pow2_invx[:, c].bitcast(U32), pow2_inv15[:, c].bitcast(U32), EXP_BITS, None,
                                        ALU.bitwise_and).then_inc(scale_step, 1)
                dve.wait_ge(scale_step, 5 * i + 5)
                nc.vector.tensor_scalar(down[:, c], pow2[:, c], 1.0 / (W_SCALE * H_SCALE), None, ALU.mult).then_inc(down_done, 1)
                nc.vector.tensor_scalar(up[:, c], pow2_invx[:, c], W_SCALE, None, ALU.mult).then_inc(scale_done, 1)

            def projection_scales(j, i):
                dve.wait_ge(down_done, i + 1)
                nc.vector.tensor_scalar(undo[:, j:j + 1], down[:, j:j + 1], 1.0 / P_SCALE, None, ALU.mult).then_inc(undo_done, 1)
                if j < 2:
                    dve.wait_ge(scale_done, i + 1)
                    nc.vector.tensor_scalar(redo[:, j:j + 1], up[:, j:j + 1], H_SCALE * P_SCALE, None, ALU.mult).then_inc(redo_done, 1)
                    dve.wait_ge(redo_done, j + 1)
                    nc.vector.tensor_scalar(bqk_up[:, j, :], bqk[:, j, :], redo[:, j:j + 1], None, ALU.mult).then_inc(bias_done, 1)

            def w_rest(j, i):
                dve.wait_ge(heads_done, i + 1)
                nc.vector.scalar_tensor_tensor(w16[:, j, 1, :, :].rearrange("p c n -> p (c n)"),
                                               w_raw[:, j, :, :].rearrange("p c n -> p (c n)"), up[:, j:j + 1],
                                               w16[:, j, 0, :, :].rearrange("p c n -> p (c n)"),
                                               ALU.mult, ALU.subtract).then_inc(rests_done, 1)

            moments(0)
            dve.wait_ge(adj_loaded, 16)
            nc.vector.tensor_reduce(peak[:, 3:4], adj_sb[:, :], AX.X, ALU.max, apply_absolute_value=True).then_inc(peak_done, 1)
            moments(1)
            scales_of(0)
            moments(2)
            dve.wait_ge(scale_done, 1)
            dve.wait_ge(heads_done, 1)
            nc.vector.scalar_tensor_tensor(adjT[:, 1, :], proj[:, A_BANK, 0:P], up[:, 3:4], adjT[:, 0, :],
                                           ALU.mult, ALU.subtract).then_inc(rests_done, 1)
            nc.vector.tensor_scalar(mask8[:, :], adj_sb[:, :], 0.0, -8e9, ALU.is_equal, ALU.mult).then_inc(mask_done, 1)
            nc.vector.memset(v16[:, 0, :, :, :, HD:VW].rearrange("p a g h e -> p (a g h) e"), 1.0).then_inc(mask_done, 1)
            moments(3)
            dve.wait_ge(bias_loaded, 64)
            nc.vector.tensor_reduce(bqk_peak[:, :], bqk[:, :, :], AX.X, ALU.max, apply_absolute_value=True).then_inc(w_peak_done, 1)
            adjacency_out(0, 0)
            w_peak_of(0, 1)
            adjacency_out(0, 1)
            scales_of(1)
            adjacency_out(0, 2)
            w_peak_of(2, 2)
            w_rest(0, 1)
            projection_scales(0, 1)
            adjacency_out(0, 3)
            moments(4)
            scales_of(2)
            w_peak_of(1, 3)
            w_rest(2, 2)
            projection_scales(2, 2)
            moments(5)
            scales_of(3)
            projection_scales(1, 3)
            dve.wait_ge(mask_done, 2)
            dve.wait_ge(undo_done, 3)

            def k_rest():
                w_rest(1, 3)
                nc.vector.tensor_tensor(score_scale[:, :], undo[:, 0:1], undo[:, 1:2], ALU.mult).then_inc(score_scale_done, 1)
                dve.wait_ge(score_scale_done, 1)

            def slot(base, k):
                softmax_shift(base, k - ATTN_BEHIND)
                v_rest(base, k - 1)
                stats_of(base, k + MOMENTS_AHEAD)
                moments_wait(base, k + MOMENTS_AHEAD)
                adjacency_out(base, k + PREP_AHEAD)
                moments_of(base, k + MOMENTS_AHEAD)
                probs_rest(base, k - ATTN_BEHIND)
                attention_out(base, k - OUT_BEHIND)

            slots(dve, slot, after_first=k_rest)
            v_rest(B, -1)
            softmax_shift(*TAIL[0], pairs_of_banks[0])
            for i, (base, k) in enumerate(TAIL):
                if i + 1 < len(TAIL):
                    softmax_shift(*TAIL[i + 1], pairs_of_banks[(i + 1) % 2])
                probs_rest(base, k)
                attention_out(base, k - 1)
            attention_out(*TAIL[-1])

        @block.tensor
        def _(pe):
            PAIRS = ((0, 0), (0, 1), (1, 0))

            def adjacency(base, k):
                if in_range(base, k):
                    pe.wait_ge(h_rest_done, base + k + 1)
                    wait(pe, a_evac, base + k)
                    for i, (s, t) in enumerate(PAIRS):
                        last = nc.tensor.matmul(proj[:, A_BANK, :], adjT[:, s, :], h16[:, k % 4, t, :],
                                                start=(i == 0), stop=(i == 2))
                    last.then_inc(a_ready, 1)

            def qk_chunk(base, k, u):
                if in_range(base, k):
                    if u == 0:
                        for i in range(GROUP):
                            wait_transposed(pe, base, k + i)
                    if isinstance(base, int) and base == 0 and k < GROUP:
                        pe.wait_ge(rests_done, 2 if u < KC else 4)
                    wait(pe, qk_evac, 2 * (base + k) - 1 + u % 2)
                    j, col = u // KC, u % KC
                    for c in range(KC):
                        for i, (s, t) in enumerate(PAIRS):
                            last = nc.tensor.matmul(proj[:, u % 2, :], w16[:, j, s, c, col * P:(col + 1) * P],
                                                    hT[:, k // GROUP % 2, t, c, :, :].rearrange("p g n -> p (g n)"),
                                                    start=(c == 0 and i == 0), stop=(c == KC - 1 and i == 2))
                    last.then_inc(qk_ready, 1)

            def v_rows(base, k):
                if in_range(base, k):
                    if isinstance(base, int) and base + k == 0:
                        pe.wait_ge(rests_done, 3)
                    wait(pe, v_evac, base + k)
                    for c in range(KC):
                        for i, (s, t) in enumerate(PAIRS):
                            last = nc.tensor.matmul(proj[:, V_BANK, :], hT[:, k // GROUP % 2, s, c, k % GROUP, :],
                                                    w16[:, 2, t, c, :], start=(c == 0 and i == 0),
                                                    stop=(c == KC - 1 and i == 2))
                    last.then_inc(v_ready, 1)

            def scores(base, k, banks=sc):
                if in_range(base, k):
                    m = base + k
                    pe.wait_ge(qk_rest_done, 2 * (m - k % GROUP + GROUP))
                    if banks is sc:
                        wait(pe, masked_done, m)
                    for c in range(KC):
                        for i, (s, t) in enumerate(PAIRS):
                            for half in range(2):
                                rows = slice(half * HD, half * HD + HD)
                                last = nc.tensor.matmul(banks[:, half, c * P:(c + 1) * P],
                                                        qkT[rows, k // GROUP % 2, s, 0, c, k % GROUP, :],
                                                        qkT[rows, k // GROUP % 2, t, 1, c, k % GROUP, :],
                                                        start=(i == 0), stop=(i == 2))
                    last.then_inc(s_ready, 1)

            def probs_times_v(base, k):
                if in_range(base, k):
                    m = base + k
                    pe.wait_ge(probsT_done, (m + 1) * 16)
                    pe.wait_ge(v_evac, m + 1)
                    wait(pe, o_evac, m)
                    for h in range(H):
                        for i, (s, t) in enumerate(PAIRS):
                            w = HD if t else VW
                            last = nc.tensor.matmul(o_view[:, h // 4, h % 4, 0:w], probsT[:, s, h % 2 * 4 + h // 2, :],
                                                    v16[:, t, k // GROUP % 2, k % GROUP, h, 0:w],
                                                    start=(i == 0), stop=(i == 2))
                    last.then_inc(o_ready, 1)

            pe.wait_ge(ident_step, 2)
            pe.wait_ge(adj_loaded, 16)
            nc.tensor.transpose(proj[:, A_BANK, 0:P], adj_sb[:, :], ident[:, :]).then_inc(adjT_ready, 1)
            pe.wait_ge(rests_done, 1)
            for k in range(PREP_AHEAD):
                adjacency(0, k)

            def slot(base, k):
                u = 2 * (k % GROUP)
                scores(base, k - ATTN_BEHIND)
                qk_chunk(base, k, u)
                qk_chunk(base, k, u + 1)
                probs_times_v(base, k - OUT_BEHIND)
                adjacency(base, k + PREP_AHEAD)
                v_rows(base, k)

            slots(pe, slot)
            scores(*TAIL[0])
            pe.wait_ge(qk_evac, 2 * B)
            scores(*TAIL[1], pairs_of_banks[1])
            probs_times_v(B, -OUT_BEHIND)
            for i, (base, k) in enumerate(TAIL):
                if i + 2 < len(TAIL):
                    pe.wait_ge(masked_done, base + k + 1)
                    scores(*TAIL[i + 2], pairs_of_banks[i % 2])
                probs_times_v(base, k)


_INS = ["x", "adj", "L0_gnn_b", "L1_gnn_Wq", "L1_gnn_bq", "L1_gnn_Wk", "L1_gnn_bk", "L1_gnn_Wv", "L1_gnn_bv"]


def kernel(**inputs):
    import concourse.bacc as _bacc
    from concourse.bass_utils import run_bass_kernel_spmd as _run

    nc = _bacc.Bacc("TRN2", target_bir_lowering=False, num_devices=1)
    arrays, args = {}, []
    for name in _INS:
        a = np.ascontiguousarray(inputs[name])
        arrays[f"in_{name}"] = a
        args.append(nc.dram_tensor(f"in_{name}", a.shape, mybir.dt.from_np(a.dtype), kind="ExternalInput").ap())
    out = nc.dram_tensor("out_x", inputs["x"].shape, F32, kind="ExternalOutput").ap()
    graph_layers(nc, *args, out)
    r = _run(nc, [arrays], core_ids=[0])
    return r.results[0]["out_x"]
```
